# Optimizing a Trainium2 kernel written in Bass

```python
import numpy as np
import jax
import jax.numpy as jnp

def _softmax(x, axis=-1):
    return jax.nn.softmax(x, axis=axis)

def _gelu(x):
    return jax.nn.gelu(x, approximate=True)

def _silu(x):
    return jax.nn.silu(x)

def _sigmoid(x):
    return jax.nn.sigmoid(x)

def _layernorm(x, axis=-1, eps=1e-05):
    m = jnp.mean(x, axis=axis, keepdims=True)
    v = jnp.var(x, axis=axis, keepdims=True)
    return (x - m) / jnp.sqrt(v + eps)

def _scatter_add(tgt, idx, src, axis=0):
    return tgt.at[idx].add(src)

def _segment_sum(src, seg, n):
    return jax.ops.segment_sum(src, seg, n)
kernel_name = 'mk_adaln_ffn_d1_seqx_r8_59a6c9'

def setup_inputs(seed: int=0):
    np.random.seed(seed)
    _w = jnp.asarray

    def _rec_inputs():
        import jax
        import jax.numpy as jnp
        _rk = jax.random.key(seed)
        x = 7.22e-05 + 1 * jax.random.normal(jax.random.fold_in(_rk, 1), (16, 128, 128), jnp.float32)
        _lenS = 128 - jax.random.randint(jax.random.fold_in(_rk, 7), (16,), 0, max(1, 128 // 4) + 1, jnp.int32)
        _lenS2 = 128 - jax.random.randint(jax.random.fold_in(_rk, 8), (16,), 0, max(1, 128 // 4) + 1, jnp.int32)
        cond_64 = -0.104238 + 1.01173 * jax.random.normal(jax.random.fold_in(_rk, 11), (16, 64), jnp.float32)
        return (x, cond_64)
    x, cond_64 = _rec_inputs()

    def _L0_cond_setup():
        import jax, jax.numpy as jnp
        import numpy as np
        B, S, H = (4, 256, 128)
        E = 8
        M = 64
        K = 2
        N_SHARED = 2
        SM = M * N_SHARED
        G = 64
        GE_TEMP = 1.0
        ALPHA = 0.001
        SEQ_AUX = True
        NORM_TOPK = True
        COS_TEMP = 0.78
        CONS_ALPHA = 0.01
        LEAKY_SLOPE = 0.01
        EPS_COS = 1e-08

        def _leaky(x):
            return jnp.where(x >= 0, x, LEAKY_SLOPE * x)

        def _moe_forward(hidden_states, g, wt, wg, w_gate, w_up, w_down, sw_gate, sw_up, sw_down):
            b, s, h = hidden_states.shape
            x = hidden_states.reshape(-1, h)
            T = x.shape[0]
            logits_h = x @ wt.T
            logits_g = g @ wg.T
            logits_g = jnp.repeat(logits_g, s, axis=0)
            logits = (logits_h + logits_g / GE_TEMP) / (1.0 + 1.0 / GE_TEMP)
            scores = jax.nn.softmax(logits, axis=-1)
            topk_w, topk_idx = jax.lax.top_k(scores, K)
            if K > 1 and NORM_TOPK:
                topk_w = topk_w / (topk_w.sum(-1, keepdims=True) + 1e-20)
            onehot = jax.nn.one_hot(topk_idx.reshape(b, s * K), E, dtype=jnp.float32)
            ce = onehot.sum(1) / (s * K / E)
            aux_loss = (ce * scores.reshape(b, s, E).mean(1)).sum(1).mean() * ALPHA
            gp = _leaky(jnp.einsum('th,ehm->etm', x, w_gate))
            up = jnp.einsum('th,ehm->etm', x, w_up)
            y_all = jnp.einsum('etm,emh->eth', gp * up, w_down)
            y_sel = y_all[topk_idx, jnp.arange(T)[:, None], :]
            y = (y_sel * topk_w[..., None]).sum(1).reshape(b, s, h)
            p = _leaky(hidden_states @ sw_gate) * (hidden_states @ sw_up) @ sw_down
            y = y + p
            num = jnp.sum(y * p, -1)
            den = jnp.maximum(jnp.linalg.norm(y, axis=-1), EPS_COS) * jnp.maximum(jnp.linalg.norm(p, axis=-1), EPS_COS)
            closs = CONS_ALPHA * jnp.mean(num / den / (1.0 + COS_TEMP))
            return (y, aux_loss + closs)
        key = jax.random.key(seed)
        ks = jax.random.split(key, 12)
        sh = 1.0 / np.sqrt(H)
        sm = 1.0 / np.sqrt(M)
        ssm = 1.0 / np.sqrt(SM)
        sg = 1.0 / np.sqrt(G)
        return {'hidden_states': jax.random.normal(ks[0], (B, S, H), jnp.float32), 'g': jax.random.normal(ks[1], (B, G), jnp.float32), 'wt': jax.random.uniform(ks[2], (E, H), jnp.float32, -sh, sh), 'wg': jax.random.uniform(ks[3], (E, G), jnp.float32, -sg, sg), 'w_gate': jax.random.uniform(ks[4], (E, H, M), jnp.float32, -sh, sh), 'w_up': jax.random.uniform(ks[5], (E, H, M), jnp.float32, -sh, sh), 'w_down': jax.random.uniform(ks[6], (E, M, H), jnp.float32, -sm, sm), 'sw_gate': jax.random.uniform(ks[7], (H, SM), jnp.float32, -sh, sh), 'sw_up': jax.random.uniform(ks[8], (H, SM), jnp.float32, -sh, sh), 'sw_down': jax.random.uniform(ks[9], (SM, H), jnp.float32, -ssm, ssm)}
    _L0_cond_all = _L0_cond_setup()
    _L0_cond_in = {k: v for k, v in _L0_cond_all.items() if k in ('wt', 'wg', 'w_gate', 'w_up', 'w_down', 'sw_gate', 'sw_up', 'sw_down')}
    del _L0_cond_all

    def _L0_ffn_setup():
        import jax, jax.numpy as jnp
        import numpy as np
        N_BLOCKS = 16
        BLOCK = 32
        TOP_K = N_BLOCKS // 4
        key = jax.random.key(seed)
        ks = jax.random.split(key, 7)
        D, H = (128, 512)
        s = lambda k, shape, scale: jax.random.normal(k, shape, dtype=jnp.float32) * scale
        return {'x': s(ks[0], (4, 512, D), 1.0), 'w_router': s(ks[1], (D, N_BLOCKS), 0.03), 'b_router': s(ks[2], (N_BLOCKS,), 0.01), 'w1': s(ks[3], (H, D), 0.03), 'b1': s(ks[4], (H,), 0.01), 'w2': s(ks[5], (D, H), 0.03), 'b2': s(ks[6], (D,), 0.01)}
    _L0_ffn_all = _L0_ffn_setup()
    _L0_ffn_in = {k: v for k, v in _L0_ffn_all.items() if k in ('w_router', 'b_router', 'w1', 'b1', 'w2', 'b2')}
    del _L0_ffn_all
    return {'x': x, 'cond_64': cond_64, 'L0_cond_wt': _L0_cond_in['wt'], 'L0_cond_wg': _L0_cond_in['wg'], 'L0_cond_w_gate': _L0_cond_in['w_gate'], 'L0_cond_w_up': _L0_cond_in['w_up'], 'L0_cond_w_down': _L0_cond_in['w_down'], 'L0_cond_sw_gate': _L0_cond_in['sw_gate'], 'L0_cond_sw_up': _L0_cond_in['sw_up'], 'L0_cond_sw_down': _L0_cond_in['sw_down'], 'L0_ffn_w_router': _L0_ffn_in['w_router'], 'L0_ffn_b_router': _L0_ffn_in['b_router'], 'L0_ffn_w1': _L0_ffn_in['w1'], 'L0_ffn_b1': _L0_ffn_in['b1'], 'L0_ffn_w2': _L0_ffn_in['w2'], 'L0_ffn_b2': _L0_ffn_in['b2']}

def reference(x, cond_64, L0_cond_wt, L0_cond_wg, L0_cond_w_gate, L0_cond_w_up, L0_cond_w_down, L0_cond_sw_gate, L0_cond_sw_up, L0_cond_sw_down, L0_ffn_w_router, L0_ffn_b_router, L0_ffn_w1, L0_ffn_b1, L0_ffn_w2, L0_ffn_b2):
    import jax
    import jax.numpy as jnp

    def _L0_cond_ref(hidden_states, g, wt, wg, w_gate, w_up, w_down, sw_gate, sw_up, sw_down):
        import jax, jax.numpy as jnp
        import numpy as np
        B, S, H = (4, 256, 128)
        E = 8
        M = 64
        K = 2
        N_SHARED = 2
        SM = M * N_SHARED
        G = 64
        GE_TEMP = 1.0
        ALPHA = 0.001
        SEQ_AUX = True
        NORM_TOPK = True
        COS_TEMP = 0.78
        CONS_ALPHA = 0.01
        LEAKY_SLOPE = 0.01
        EPS_COS = 1e-08

        def _leaky(x):
            return jnp.where(x >= 0, x, LEAKY_SLOPE * x)

        def _moe_forward(hidden_states, g, wt, wg, w_gate, w_up, w_down, sw_gate, sw_up, sw_down):
            b, s, h = hidden_states.shape
            x = hidden_states.reshape(-1, h)
            T = x.shape[0]
            logits_h = x @ wt.T
            logits_g = g @ wg.T
            logits_g = jnp.repeat(logits_g, s, axis=0)
            logits = (logits_h + logits_g / GE_TEMP) / (1.0 + 1.0 / GE_TEMP)
            scores = jax.nn.softmax(logits, axis=-1)
            topk_w, topk_idx = jax.lax.top_k(scores, K)
            if K > 1 and NORM_TOPK:
                topk_w = topk_w / (topk_w.sum(-1, keepdims=True) + 1e-20)
            onehot = jax.nn.one_hot(topk_idx.reshape(b, s * K), E, dtype=jnp.float32)
            ce = onehot.sum(1) / (s * K / E)
            aux_loss = (ce * scores.reshape(b, s, E).mean(1)).sum(1).mean() * ALPHA
            gp = _leaky(jnp.einsum('th,ehm->etm', x, w_gate))
            up = jnp.einsum('th,ehm->etm', x, w_up)
            y_all = jnp.einsum('etm,emh->eth', gp * up, w_down)
            y_sel = y_all[topk_idx, jnp.arange(T)[:, None], :]
            y = (y_sel * topk_w[..., None]).sum(1).reshape(b, s, h)
            p = _leaky(hidden_states @ sw_gate) * (hidden_states @ sw_up) @ sw_down
            y = y + p
            num = jnp.sum(y * p, -1)
            den = jnp.maximum(jnp.linalg.norm(y, axis=-1), EPS_COS) * jnp.maximum(jnp.linalg.norm(p, axis=-1), EPS_COS)
            closs = CONS_ALPHA * jnp.mean(num / den / (1.0 + COS_TEMP))
            return (y, aux_loss + closs)
        y, _ = _moe_forward(hidden_states, g, wt, wg, w_gate, w_up, w_down, sw_gate, sw_up, sw_down)
        return y

    def _L0_ffn_ref(x, w_router, b_router, w1, b1, w2, b2):
        import jax, jax.numpy as jnp
        import numpy as np
        N_BLOCKS = 16
        BLOCK = 32
        TOP_K = N_BLOCKS // 4
        orig_shape = x.shape
        D = orig_shape[-1]
        xf = x.reshape(-1, D)
        prob = jax.nn.softmax(xf @ w_router + b_router, axis=-1)
        _, idx = jax.lax.top_k(prob, TOP_K)
        mask = (idx[:, :, None] == jnp.arange(N_BLOCKS)[None, None, :]).any(axis=1)
        mask = mask.astype(x.dtype)
        w1b = w1.reshape(N_BLOCKS, BLOCK, D)
        b1b = b1.reshape(N_BLOCKS, BLOCK)
        w2b = jnp.transpose(w2.reshape(D, N_BLOCKS, BLOCK), (1, 2, 0))
        h = jax.nn.relu(jnp.einsum('nd,ebd->neb', xf, w1b) + b1b[None])
        y = jnp.einsum('neb,ebd,ne->nd', h, w2b, mask)
        y = y + b2[None, :]
        return y.reshape(orig_shape)
    x = x + _L0_ffn_ref(_L0_cond_ref(x, cond_64, L0_cond_wt, L0_cond_wg, L0_cond_w_gate, L0_cond_w_up, L0_cond_w_down, L0_cond_sw_gate, L0_cond_sw_up, L0_cond_sw_down), L0_ffn_w_router, L0_ffn_b_router, L0_ffn_w1, L0_ffn_b1, L0_ffn_w2, L0_ffn_b2)
    return x

_drawn_inputs = setup_inputs


def setup_inputs(seed=0):
    import zlib

    import numpy as np

    out = dict(_drawn_inputs(seed))
    spreads = {}
    factors = {'cond_64': 6.856,
     'L0_cond_wt': 6.63,
     'L0_cond_wg': 6.896,
     'L0_cond_w_gate': 6.073,
     'L0_cond_w_up': 5.474,
     'L0_cond_w_down': 5.494,
     'L0_cond_sw_gate': 5.087,
     'L0_cond_sw_up': 4.745,
     'L0_cond_sw_down': 4.731,
     'L0_ffn_w_router': 4.828,
     'L0_ffn_b_router': 8.0,
     'L0_ffn_w1': 5.083,
     'L0_ffn_b1': 200.0,
     'L0_ffn_w2': 4.16,
     'L0_ffn_b2': 200.0}
    for name, (base, spread) in spreads.items():
        noise = np.random.default_rng([zlib.crc32(name.encode()), seed]).standard_normal(out[name].shape)
        drawn = base * np.exp(spread * noise) if base else spread * noise
        out[name] = jnp.asarray(drawn.astype(out[name].dtype))
    for name, factor in factors.items():
        out[name] = (out[name] * factor).astype(out[name].dtype)
    return out
```

```python
from contextlib import ExitStack

import concourse.bass as bass
from concourse import mybir

N_TOK, D, E, M, G, B = 2048, 128, 8, 64, 64, 16
HID, NB = 512, 16
TOKENS = 512
GROUPS = N_TOK // TOKENS
TILES = N_TOK // 128
TG = TOKENS // 128
EC = E * M // 128
MC = EC + 1
FC = HID // 128
TOP2 = 4
PAD = 8 - TOP2
PENALTY = -(2.0 ** 127)
TINY = 2.0 ** -126


def build(nc: bass.Bass, x_t, w_in, w_down, w1_t, w2_t, wt_t, wg_t, cond_t, b_router, b1, b2,
          const_rows, const_sel, out):
    SEL_W = 1 + B * E
    SEL_P = SEL_W + EC * 128
    f32, f32r = mybir.dt.float32, mybir.dt.float32r
    ALU, ACT, AX = mybir.AluOpType, mybir.ActivationFunctionType, mybir.AxisListType

    ctx = ExitStack()
    with ctx:
        def sb(name, shape, dt=f32):
            return ctx.enter_context(nc.sbuf_tensor(name, shape, dt))

        def sem(name):
            return ctx.enter_context(nc.semaphore(name))

        x_raw = sb("x_raw", [128, N_TOK])
        win_raw = sb("win_raw", [128, 2 * MC * 128])
        wdn_raw = sb("wdn_raw", [128, MC * 128])
        w1_raw = sb("w1_raw", [128, HID])
        w2_raw = sb("w2_raw", [128, HID])
        wt_sb = sb("wt_sb", [128, E])
        wg_sb = sb("wg_sb", [G, E])
        cond_sb = sb("cond_sb", [G, B])
        wr_raw = sb("wr_raw", [128, NB])
        br_sb = sb("br_sb", [1, NB])
        b2_sb = sb("b2_sb", [128, 1])
        rows_sb = sb("rows_sb", [128, 128 + E])
        ident, iota = rows_sb[:, 0:128], rows_sb[:, 128:128 + E]
        sel_raw = sb("sel_raw", [NB + 2, 128 + 2 * HID + 1])
        x_hi, x_lo = sb("x_hi", [128, N_TOK], f32r), sb("x_lo", [128, N_TOK], f32r)
        win_hi, win_lo = sb("win_hi", [128, 2 * MC * 128], f32r), sb("win_lo", [128, 2 * MC * 128], f32r)
        wdn_hi, wdn_lo = sb("wdn_hi", [128, MC * 128], f32r), sb("wdn_lo", [128, MC * 128], f32r)
        w1_hi, w1_lo = sb("w1_hi", [128, HID], f32r), sb("w1_lo", [128, HID], f32r)
        w2_hi, w2_lo = sb("w2_hi", [128, HID], f32r), sb("w2_lo", [128, HID], f32r)
        wr_hi, wr_lo = sb("wr_hi", [128, NB], f32r), sb("wr_lo", [128, NB], f32r)
        sel_w = sb("sel_w", [2 * E, EC * 128], f32r)
        sel_p = sb("sel_p", [NB + 2, HID], f32r)
        sel_hi = sb("sel_hi", [NB + 2, HID], f32r)
        w_tok = sb("w_tok", [128, TILES, 2 * E], f32r)
        w_row = sb("w_row", [2 * E, N_TOK], f32r)
        pen_row = sb("pen_row", [NB + 2, TOKENS], f32r)
        h_hi, h_lo = sb("h_hi", [128, MC, TOKENS], f32r), sb("h_lo", [128, MC, TOKENS], f32r)
        y_hi, y_lo = sb("y_hi", [128, TOKENS], f32r), sb("y_lo", [128, TOKENS], f32r)
        r_hi, r_lo = sb("r_hi", [128, FC, TOKENS], f32r), sb("r_lo", [128, FC, TOKENS], f32r)
        ones = sb("ones", [16, 128])
        bdiag = sb("bdiag", [B, B, E])
        leak = sb("leak", [128, MC, TOKENS])
        act_g = sb("act_g", [128, MC, TOKENS])
        gu = sb("gu", [128, EC, TOKENS])
        h = sb("h", [128, MC, TOKENS])
        y_out = sb("y_out", [128, N_TOK])
        mx1, z1, rank1, m2nd, rank2, den = (sb(n, [128, TILES]) for n in ("mx1", "z1", "rank1", "m2nd", "rank2", "den"))
        d1, e1, v1, first, e1b, v2, second, wun, wgt = (
            sb(n, [128, TILES, E]) for n in ("d1", "e1", "v1", "first", "e1b", "v2", "second", "wun", "wgt"))
        mx2, z2, rz2 = (sb(n, [128, TG]) for n in ("mx2", "z2", "rz2"))
        d2, e2, s2 = (sb(n, [128, TG, NB]) for n in ("d2", "e2", "s2"))
        cand = sb("cand", [128, TG, NB + PAD])
        rest = sb("rest", [128, TG, NB + PAD])
        top8 = sb("top8", [128, TG, 8])
        pen = sb("pen", [128, TG, NB])

        bank = [ctx.enter_context(nc.psum_tensor(f"bank{i}", [128, TOKENS], f32)) for i in range(8)]
        w_bank, y_bank, o_bank = bank[4:6], bank[6], bank[7]
        z_bank = [bank[2], bank[3], bank[0], bank[1]]
        logit1 = bank[4][:, 0:TILES * E].rearrange("p (t e) -> p t e", e=E)
        logit2 = y_bank[:, 0:TG * NB].rearrange("p (t e) -> p t e", e=NB)

        x_in = [sem(f"x_in{g}") for g in range(GROUPS)]
        win_in = [sem(f"win_in{c}") for c in range(2)]
        small_in, wdn_in, w1_in, w2_in = (sem(n) for n in ("small_in", "wdn_in", "w1_in", "w2_in"))
        x_hi_ready, x_lo_ready = sem("x_hi_ready"), sem("x_lo_ready")
        w_hi_ready, w_lo_ready = sem("w_hi_ready"), sem("w_lo_ready")
        ones_ready, sel_ready, sel_hi_ready, sel_p_ready, pad_ready = (sem(n) for n in (
            "ones_ready", "sel_ready", "sel_hi_ready", "sel_p_ready", "pad_ready"))
        lg_ready, bdiag_ready, logit1_ready, d1_ready, e1_ready = (sem(n) for n in (
            "lg_ready", "bdiag_ready", "logit1_ready", "d1_ready", "e1_ready"))
        w_tok_ready, w_turned, w_row_ready = sem("w_tok_ready"), sem("w_turned"), sem("w_row_ready")
        g_ready, u_ready, wb_ready, y_ready, z_ready, o_ready, logit2_ready, pen_turned = (sem(n) for n in (
            "g_ready", "u_ready", "wb_ready", "y_ready", "z_ready", "o_ready", "logit2_ready", "pen_turned"))
        leak_ready, h_hi_ready, y_hi_ready, r_hi_ready, e2_ready, pen_row_ready = (sem(n) for n in (
            "leak_ready", "h_hi_ready", "y_hi_ready", "r_hi_ready", "e2_ready", "pen_row_ready"))
        act_g_done, gu_done, h_done, y_lo_ready, r_lo_ready, out_done, d2_ready, pen_ready = (sem(n) for n in (
            "act_g_done", "gu_done", "h_done", "y_lo_ready", "r_lo_ready", "out_done", "d2_ready", "pen_ready"))
        h_lo_ready, step1, step2, stored = sem("h_lo_ready"), sem("step1"), sem("step2"), sem("stored")

        half = 4 * 128
        pieces = [(win_raw[:, 0:half], win_hi[:, 0:half], win_lo[:, 0:half], win_in[0], 16),
                  (win_raw[:, half:], win_hi[:, half:], win_lo[:, half:], win_in[1], 16),
                  (wdn_raw[:, :], wdn_hi[:, :], wdn_lo[:, :], wdn_in, 16),
                  (wr_raw[:, :], wr_hi[:, :], wr_lo[:, :], small_in, SMALL),
                  (w1_raw[:, :], w1_hi[:, :], w1_lo[:, :], w1_in, 16),
                  (w2_raw[:, :], w2_hi[:, :], w2_lo[:, :], w2_in, 16)]

        def group(t, g):
            return t[:, bass.ts(g, TOKENS)]

        block = ctx.enter_context(nc.Block())

        @block.sync
        def _(sp):
            sp.dma_start(x_raw[:, 0:TOKENS], x_t[:, 0:TOKENS]).then_inc(x_in[0], 16)
            sp.dma_start(win_raw[:, 0:half], w_in[:, 0:half]).then_inc(win_in[0], 16)
            for g in range(1, GROUPS):
                sp.dma_start(x_raw[:, g * TOKENS:(g + 1) * TOKENS],
                             x_t[:, g * TOKENS:(g + 1) * TOKENS]).then_inc(x_in[g], 16)
            sp.dma_start(win_raw[:, half:], w_in[:, half:]).then_inc(win_in[1], 16)
            sp.dma_start(wdn_raw[:, :], w_down).then_inc(wdn_in, 16)
            sp.dma_start(w1_raw[:, :], w1_t).then_inc(w1_in, 16)
            sp.dma_start(w2_raw[:, :], w2_t).then_inc(w2_in, 16)

            def store(f):
                sp.wait_ge(out_done, f + 1)
                sp.dma_start(group(out, f), group(y_out, f)).then_inc(stored, 16)

            with sp.Fori(0, GROUPS) as f:
                store(f)
            sp.wait_ge(stored, 16 * GROUPS)

        @block.gpsimd
        def _(pool):
            nc.gpsimd.memset(ones[:, :], 1.0).then_inc(ones_ready, 1)
            nc.gpsimd.memset(pen_row[:, :].bitcast(f32), 1.0).then_inc(ones_ready, 1)
            nc.gpsimd.memset(cand[:, :, NB:], -1.0).then_inc(pad_ready, 1)

            def x_low(g):
                pool.wait_ge(x_hi_ready, g + 1)
                nc.gpsimd.tensor_tensor(group(x_lo, g), group(x_raw, g), group(x_hi, g).bitcast(f32),
                                        ALU.subtract).then_inc(x_lo_ready, 1)

            x_low(0)

            def experts(g):
                for c in range(MC):
                    pool.wait_ge(h_hi_ready, MC * g + c + 1)
                    nc.gpsimd.tensor_tensor(h_lo[:, c, :], h[:, c, :], h_hi[:, c, :].bitcast(f32),
                                            ALU.subtract).then_inc(h_lo_ready, 1)

            for g in range(1, GROUPS):
                x_low(g)
            with pool.Fori(0, GROUPS) as g:
                experts(g)

        @block.scalar
        def _(act):
            act.dma_start(cond_sb[:, :], cond_t).then_inc(small_in, 16)
            act.dma_start(wg_sb[:, :], wg_t).then_inc(small_in, 16)
            act.dma_start(wt_sb[:, :], wt_t[:, 0:E]).then_inc(small_in, 16)
            act.dma_start(rows_sb[:, :], const_rows).then_inc(small_in, 16)
            act.dma_start(sel_raw[:, 0:SEL_P], const_sel[:, 0:SEL_P]).then_inc(small_in, 16)
            act.dma_start(sel_raw[0:NB, SEL_P:], const_sel[0:NB, SEL_P:]).then_inc(small_in, 16)
            act.dma_start(sel_raw[NB:, SEL_P:], b1.to_broadcast([2, HID])).then_inc(small_in, 16)
            act.dma_start(wr_raw[:, :], wt_t[:, E:]).then_inc(small_in, 16)
            act.dma_start(br_sb[:, :], b_router).then_inc(small_in, 16)
            act.dma_start(b2_sb[:, :], b2).then_inc(small_in, 16)

            def x_high(g):
                act.wait_ge(x_in[g], 16)
                nc.scalar.activation(x_hi[:, g * TOKENS:(g + 1) * TOKENS],
                                     x_raw[:, g * TOKENS:(g + 1) * TOKENS], ACT.Copy).then_inc(x_hi_ready, 1)

            def w_high(n):
                raw, hi, _, loaded, value = pieces[n]
                act.wait_ge(loaded, value)
                nc.scalar.activation(hi, raw, ACT.Copy).then_inc(w_hi_ready, 1)

            x_high(0)
            w_high(0)
            act.wait_ge(d1_ready, 1)
            nc.scalar.activation(e1[:, :, :], d1[:, :, :], ACT.Exp, scale=0.5).then_inc(e1_ready, 1)
            act.wait_ge(small_in, SMALL)
            nc.scalar.activation(sel_w[:, :], sel_raw[0:2 * E, SEL_W:SEL_P], ACT.Copy).then_inc(sel_ready, 1)
            w_high(1)
            nc.scalar.activation(sel_hi[:, :], sel_raw[:, SEL_P:],
                                 ACT.Copy).then_inc(sel_hi_ready, 1)

            def w_rows(g):
                act.wait_ge(w_turned, g + 1)
                nc.scalar.activation(w_row[:, g * TOKENS:(g + 1) * TOKENS],
                                     bank[4 + g][0:2 * E, :], ACT.Copy).then_inc(w_row_ready, 1)

            def leaks(g, c):
                act.wait_ge(g_ready, MC * g + c + 1)
                nc.scalar.activation(leak[:, c, :], bank[2 * (c % 2)][:, :], ACT.Copy,
                                     scale=0.01).then_inc(leak_ready, 1)

            def h_high(g, c):
                if c == EC:
                    act.wait_ge(gu_done, MC * (g + 1))
                else:
                    act.wait_ge(h_done, EC * g + c + 1)
                nc.scalar.activation(h_hi[:, c, :], h[:, c, :], ACT.Copy).then_inc(h_hi_ready, 1)

            def y_high(g):
                act.wait_ge(y_ready, g + 1)
                nc.scalar.activation(y_hi[:, :], y_bank[:, :], ACT.Copy).then_inc(y_hi_ready, 1)

            def exps(f):
                act.wait_ge(d2_ready, f + 1)
                nc.scalar.activation(e2[:, :, :], d2[:, :, :], ACT.Exp).then_inc(e2_ready, 1)

            def pen_rows(f):
                act.wait_ge(pen_turned, f + 1)
                nc.scalar.activation(pen_row[0:NB, :], y_bank[0:NB, :], ACT.Copy).then_inc(pen_row_ready, 1)

            def relus(f, c):
                act.wait_ge(z_ready, FC * f + c + 1)
                nc.scalar.activation(r_hi[:, c, :], z_bank[c][:, :], ACT.Relu).then_inc(r_hi_ready, 1)

            def body(g):
                leaks(g, 0)
                exps(g - 1)
                leaks(g, 1)
                act.wait_ge(y_ready, g)
                for c in range(2, MC):
                    h_high(g, c - 2)
                    leaks(g, c)
                h_high(g, MC - 2)
                pen_rows(g - 1)
                relus(g - 1, 0)
                h_high(g, MC - 1)
                for c in range(1, FC):
                    relus(g - 1, c)
                y_high(g)

            leaks(0, 0)
            leaks(0, 1)
            act.wait_ge(ones_ready, 2)
            for g in range(GROUPS):
                w_rows(g)
            w_high(2)
            for c in range(2, MC):
                h_high(0, c - 2)
                leaks(0, c)
                x_high(c - 1)
            h_high(0, MC - 2)
            w_high(3)
            w_high(4)
            h_high(0, MC - 1)
            w_high(5)
            y_high(0)
            with act.Fori(1, GROUPS) as g:
                body(g)
            exps(GROUPS - 1)
            pen_rows(GROUPS - 1)
            for c in range(FC):
                relus(GROUPS - 1, c)

        @block.vector
        def _(dve):
            def w_low(n):
                raw, hi, lo, _, _ = pieces[n]
                dve.wait_ge(w_hi_ready, n + 1)
                nc.vector.tensor_tensor(lo, raw, hi.bitcast(f32), ALU.subtract).then_inc(w_lo_ready, 1)

            def spread(t, n):
                return t[:, :].unsqueeze(2).to_broadcast([128, t.shape[1], n])

            dve.wait_ge(lg_ready, 1)
            nc.vector.tensor_tensor(bdiag[:, :, :], o_bank[0:B, 0:E].unsqueeze(1).to_broadcast([B, B, E]),
                                    sel_raw[0:B, 1:SEL_W].rearrange("p (t e) -> p t e", e=E),
                                    ALU.mult).then_inc(bdiag_ready, 1)
            w_low(0)
            steps = [0]

            def step(instruction):
                steps[0] += 1
                instruction.then_inc(step1, 1)
                dve.wait_ge(step1, steps[0])

            v = nc.vector
            dve.wait_ge(logit1_ready, 1)
            step(v.reduce_max(mx1[:, :], logit1, AX.X))
            v.tensor_tensor(d1[:, :, :], logit1, spread(mx1, E), ALU.subtract).then_inc(d1_ready, 1)
            dve.wait_ge(d1_ready, 1)
            step(v.scalar_tensor_tensor(v1[:, :, :], d1[:, :, :], 0.0,
                                        iota.unsqueeze(1).to_broadcast([128, TILES, E]), ALU.is_ge, ALU.mult))
            step(v.reduce_max(rank1[:, :], v1[:, :, :], AX.X))
            step(v.tensor_tensor(first[:, :, :], v1[:, :, :], spread(rank1, E), ALU.is_equal))
            dve.wait_ge(e1_ready, 1)
            v.reduce_sum(z1[:, :], e1[:, :, :], AX.X)
            step(v.scalar_tensor_tensor(e1b[:, :, :], first[:, :, :], -2.0, e1[:, :, :], ALU.mult, ALU.add))
            step(v.reduce_max(m2nd[:, :], e1b[:, :, :], AX.X))
            step(v.tensor_tensor(v2[:, :, :], e1b[:, :, :], spread(m2nd, E), ALU.is_equal))
            step(v.tensor_tensor(v1[:, :, :], v2[:, :, :], iota.unsqueeze(1).to_broadcast([128, TILES, E]), ALU.mult))
            step(v.reduce_max(rank2[:, :], v1[:, :, :], AX.X))
            step(v.tensor_tensor(second[:, :, :], v1[:, :, :], spread(rank2, E), ALU.is_equal))
            step(v.scalar_tensor_tensor(den[:, :], z1[:, :], 1e-20, m2nd[:, :], ALU.mult, ALU.add))
            step(v.tensor_scalar(den[:, :], den[:, :], 1.0, None, ALU.add))
            step(v.reciprocal(den[:, :], den[:, :]))
            step(v.tensor_tensor(wun[:, :, :], second[:, :, :], spread(m2nd, E), ALU.mult))
            step(v.tensor_tensor(wun[:, :, :], wun[:, :, :], first[:, :, :], ALU.add))
            step(v.tensor_tensor(wgt[:, :, :], wun[:, :, :], spread(den, E), ALU.mult))
            step(v.tensor_copy(w_tok[:, :, 0:E], wgt[:, :, :]))
            v.tensor_tensor(w_tok[:, :, E:], wgt[:, :, :], w_tok[:, :, 0:E].bitcast(f32),
                            ALU.subtract).then_inc(w_tok_ready, 1)

            def leaky(g, c):
                dve.wait_ge(leak_ready, MC * g + c + 1)
                v.tensor_tensor(act_g[:, c, :], bank[2 * (c % 2)][:, :], leak[:, c, :],
                                ALU.max).then_inc(act_g_done, 1)

            def times_up(g, c):
                dve.wait_ge(u_ready, MC * g + c + 1)
                dve.wait_ge(act_g_done, MC * g + c + 1)
                v.tensor_tensor(h[:, c, :] if c == EC else gu[:, c, :], bank[2 * (c % 2) + 1][:, :],
                                act_g[:, c, :], ALU.mult).then_inc(gu_done, 1)

            def times_weight(g, c):
                dve.wait_ge(wb_ready, EC * g + c + 1)
                dve.wait_ge(gu_done, MC * g + c + 1)
                v.tensor_tensor(h[:, c, :], w_bank[c % 2][:, :], gu[:, c, :], ALU.mult).then_inc(h_done, 1)

            def y_low(g):
                dve.wait_ge(y_hi_ready, g + 1)
                v.tensor_tensor(y_lo[:, :], y_bank[:, :], y_hi[:, :].bitcast(f32),
                                ALU.subtract).then_inc(y_lo_ready, 1)

            def relu_low(f, c):
                dve.wait_ge(r_hi_ready, FC * f + c + 1)
                v.scalar_tensor_tensor(r_lo[:, c, :], z_bank[c][:, :], 0.0, r_hi[:, c, :].bitcast(f32),
                                       ALU.max, ALU.subtract).then_inc(r_lo_ready, 1)

            def result(f):
                dve.wait_ge(o_ready, f + 1)
                v.scalar_tensor_tensor(group(y_out, f), o_bank[:, :], b2_sb[:, :], group(x_raw, f),
                                       ALU.add, ALU.add).then_inc(out_done, 1)

            STEPS2 = 8

            def before_max(f):
                dve.wait_ge(step2, STEPS2 * f + 5)

            def before_replace(f):
                dve.wait_ge(step2, STEPS2 * f + 7)

            def pick(f, n):
                if n == 0:
                    dve.wait_ge(logit2_ready, f + 1)
                    v.reduce_max(mx2[:, :], logit2, AX.X).then_inc(step2, 1)
                elif n == 1:
                    dve.wait_ge(step2, STEPS2 * f + 1)
                    v.tensor_tensor(d2[:, :, :], logit2, spread(mx2, NB), ALU.subtract).then_inc(d2_ready, 1)
                elif n == 2:
                    dve.wait_ge(e2_ready, f + 1)
                    v.reduce_sum(z2[:, :], e2[:, :, :], AX.X).then_inc(step2, 1)
                elif n == 3:
                    dve.wait_ge(step2, STEPS2 * f + 2)
                    v.reciprocal(rz2[:, :], z2[:, :]).then_inc(step2, 1)
                elif n == 4:
                    dve.wait_ge(step2, STEPS2 * f + 3)
                    v.tensor_tensor(s2[:, :, :], e2[:, :, :], spread(rz2, NB), ALU.mult).then_inc(step2, 1)
                elif n == 5:
                    dve.wait_ge(step2, STEPS2 * f + 4)
                    v.scalar_tensor_tensor(cand[:, :, 0:NB], s2[:, :, :], TINY, s2[:, :, :],
                                           ALU.is_ge, ALU.mult).then_inc(step2, 1)
                elif n == 6:
                    for t in range(TG):
                        last = v.max(top8[:, t, :], cand[:, t, 0:NB])
                    last.then_inc(step2, 1)
                elif n == 7:
                    dve.wait_ge(step2, STEPS2 * f + 6)
                    v.memset(top8[:, :, TOP2:], -1.0).then_inc(step2, 1)
                elif n == 8:
                    for t in range(TG):
                        last = v.match_replace(rest[:, t, :], top8[:, t, :], cand[:, t, :], 2.0)
                    last.then_inc(step2, 1)
                elif n == 9:
                    dve.wait_ge(step2, STEPS2 * f + 8)
                    v.tensor_scalar(pen[:, :, :], rest[:, :, 0:NB], 2.0, PENALTY,
                                    ALU.is_lt, ALU.mult).then_inc(pen_ready, 1)

            def body(g, ffn=True):
                f = g - 1
                free = iter(range(10)) if ffn else iter(())

                def pick_next():
                    n = next(free, None)
                    if n is not None:
                        pick(f, n)

                pick_next()
                leaky(g, 0)
                pick_next()
                times_up(g, 0)
                leaky(g, 1)
                pick_next()
                if ffn:
                    dve.wait_ge(h_lo_ready, MC * g)
                times_weight(g, 0)
                pick_next()
                times_up(g, 1)
                if not ffn:
                    w_low(1)
                pick_next()
                leaky(g, 2)
                pick_next()
                times_weight(g, 1)
                if ffn:
                    before_max(f)
                times_up(g, 2)
                if not ffn:
                    w_low(2)
                pick_next()
                leaky(g, 3)
                pick_next()
                times_weight(g, 2)
                if ffn:
                    before_replace(f)
                times_up(g, 3)
                pick_next()
                leaky(g, 4)
                pick_next()
                times_weight(g, 3)
                times_up(g, 4)
                if ffn:
                    for c in range(FC):
                        relu_low(f, c)
                else:
                    for n in range(3, 6):
                        w_low(n)
                    dve.wait_ge(sel_hi_ready, 1)
                    v.scalar_tensor_tensor(sel_p[:, :], sel_hi[:, :].bitcast(f32), sel_raw[:, 0:1],
                                           sel_raw[:, SEL_P:],
                                           ALU.mult, ALU.add).then_inc(sel_p_ready, 1)
                    dve.wait_ge(pad_ready, 1)
                    dve.wait_ge(small_in, SMALL)
                y_low(g)
                if ffn:
                    result(f)

            body(0, ffn=False)
            with dve.Fori(1, GROUPS) as g:
                body(g)
            f = GROUPS - 1
            for n in range(10):
                if n == 6:
                    before_max(f)
                elif n == 8:
                    before_replace(f)
                pick(f, n)
            for c in range(FC):
                relu_low(f, c)
            result(f)

        @block.tensor
        def _(pe):
            def product(dst, w_hi, w_lo, m_hi, m_lo, start, stop):
                nc.tensor.matmul(dst, w_hi, m_hi, start=start, stop=False)
                nc.tensor.matmul(dst, w_lo, m_hi, start=False, stop=False)
                return nc.tensor.matmul(dst, w_hi, m_lo, start=False, stop=stop)

            pe.wait_ge(small_in, SMALL)
            nc.tensor.matmul(o_bank[0:B, 0:E], cond_sb[:, :], wg_sb[:, :], start=True, stop=True).then_inc(lg_ready, 1)
            for t in range(TILES):
                if t % TG == 0:
                    pe.wait_ge(x_in[t // TG], 16)
                nc.tensor.matmul(logit1[:, t, :], x_raw[:, t * 128:(t + 1) * 128], wt_sb[:, :],
                                 start=(t == 0), stop=False, skip_group_check=True)
            pe.wait_ge(bdiag_ready, 1)
            pe.wait_ge(ones_ready, 1)
            nc.tensor.matmul(bank[4][:, 0:TILES * E], ones[:, :], bdiag[:, :, :].rearrange("p t e -> p (t e)"),
                             start=False, stop=True, skip_group_check=True).then_inc(logit1_ready, 1)

            def weights_in(c, up):
                at = (2 * c + up) * 128
                return win_hi[:, at:at + 128], win_lo[:, at:at + 128]

            def gate_up(g, c):
                if c >= 2:
                    pe.wait_ge(act_g_done, MC * g + c - 1)
                product(bank[2 * (c % 2)][:, :], *weights_in(c, 0), group(x_hi, g), group(x_lo, g),
                        True, True).then_inc(g_ready, 1)
                if c >= 2:
                    pe.wait_ge(h_done, EC * g + c - 1)
                product(bank[2 * (c % 2) + 1][:, :], *weights_in(c, 1), group(x_hi, g), group(x_lo, g),
                        True, True).then_inc(u_ready, 1)

            def weight_bank(g, c):
                nc.tensor.matmul(w_bank[c % 2][:, :], sel_w[:, c * 128:(c + 1) * 128], group(w_row, g),
                                 start=True, stop=True).then_inc(wb_ready, 1)

            def down(g):
                for c in range(MC):
                    pe.wait_ge(h_hi_ready, MC * g + c + 1)
                    pe.wait_ge(h_lo_ready, MC * g + c + 1)
                    last = product(y_bank[:, :], wdn_hi[:, c * 128:(c + 1) * 128], wdn_lo[:, c * 128:(c + 1) * 128],
                                   h_hi[:, c, :], h_lo[:, c, :], c == 0, c == MC - 1)
                last.then_inc(y_ready, 1)

            def router2(g):
                pe.wait_ge(y_hi_ready, g + 1)
                pe.wait_ge(y_lo_ready, g + 1)
                for t in range(TG):
                    at = slice(t * 128, (t + 1) * 128)
                    for y, w in ((y_hi, wr_hi), (y_hi, wr_lo), (y_lo, wr_hi)):
                        nc.tensor.matmul(logit2[:, t, :], y[:, at], w[:, :], skip_group_check=True,
                                         start=(t == 0 and w is wr_hi and y is y_hi), stop=False)
                nc.tensor.matmul(logit2, ones[0:1, :], br_sb[:, :].unsqueeze(1).to_broadcast([1, TG, NB]),
                                 start=False, stop=True, skip_group_check=True).then_inc(logit2_ready, 1)

            def turn_penalties(f):
                pe.wait_ge(pen_ready, f + 1)
                for t in range(TG):
                    last = nc.tensor.transpose(y_bank[0:NB, t * 128:(t + 1) * 128], pen[:, t, :], ident)
                last.then_inc(pen_turned, 1)

            def ffn_up(f, c):
                at = slice(c * 128, (c + 1) * 128)
                product(z_bank[c][:, :], w1_hi[:, at], w1_lo[:, at], y_hi[:, :], y_lo[:, :], True, False)
                if c == 0:
                    pe.wait_ge(pen_row_ready, f + 1)
                nc.tensor.matmul(z_bank[c][:, :], sel_p[:, at], pen_row[:, :],
                                 start=False, stop=True).then_inc(z_ready, 1)

            def ffn_down(f):
                for c in range(FC):
                    at = slice(c * 128, (c + 1) * 128)
                    pe.wait_ge(r_hi_ready, FC * f + c + 1)
                    pe.wait_ge(r_lo_ready, FC * f + c + 1)
                    last = product(o_bank[:, :], w2_hi[:, at], w2_lo[:, at], r_hi[:, c, :], r_lo[:, c, :],
                                   c == 0, c == FC - 1)
                last.then_inc(o_ready, 1)

            pe.wait_ge(x_hi_ready, 1)
            pe.wait_ge(x_lo_ready, 1)
            pe.wait_ge(w_lo_ready, 1)
            gate_up(0, 0)
            gate_up(0, 1)
            pe.wait_ge(w_tok_ready, 1)
            for g in range(GROUPS):
                for t in range(TG):
                    last = nc.tensor.transpose(bank[4 + g][0:2 * E, t * 128:(t + 1) * 128],
                                               w_tok[:, g * TG + t, :].bitcast(f32), ident)
                last.then_inc(w_turned, 1)
            pe.wait_ge(w_row_ready, GROUPS)
            pe.wait_ge(sel_ready, 1)
            weight_bank(0, 0)
            weight_bank(0, 1)
            pe.wait_ge(w_lo_ready, 2)
            for c in range(2, MC):
                gate_up(0, c)
                if c < EC:
                    weight_bank(0, c)
            pe.wait_ge(w_lo_ready, 3)
            down(0)
            pe.wait_ge(w_lo_ready, 6)
            router2(0)
            pe.wait_ge(sel_p_ready, 1)
            pe.wait_ge(x_hi_ready, GROUPS)
            pe.wait_ge(x_lo_ready, GROUPS)

            def body(g):
                f = g - 1
                for c in range(MC):
                    gate_up(g, c)
                    if c < EC:
                        weight_bank(g, c)
                turn_penalties(f)
                pe.wait_ge(gu_done, MC * g + EC)
                ffn_up(f, 0)
                ffn_up(f, 1)
                pe.wait_ge(gu_done, MC * g + MC)
                ffn_up(f, 2)
                ffn_up(f, 3)
                down(g)
                ffn_down(f)
                router2(g)

            with pe.Fori(1, GROUPS) as g:
                body(g)
            f = GROUPS - 1
            turn_penalties(f)
            for c in range(FC):
                ffn_up(f, c)
            pe.wait_ge(out_done, f)
            ffn_down(f)


SMALL = 10 * 16


def kernel(x, cond_64, L0_cond_wt, L0_cond_wg, L0_cond_w_gate, L0_cond_w_up, L0_cond_w_down, L0_cond_sw_gate,
           L0_cond_sw_up, L0_cond_sw_down, L0_ffn_w_router, L0_ffn_b_router, L0_ffn_w1, L0_ffn_b1, L0_ffn_w2,
           L0_ffn_b2):
    import numpy as np
    import concourse.bacc as bacc
    from concourse.bass_utils import run_bass_kernel_spmd

    def arr(a):
        return np.asarray(a)

    def columns(w):
        return arr(w).transpose(1, 0, 2).reshape(D, E * M)

    gate = np.concatenate([columns(L0_cond_w_gate), arr(L0_cond_sw_gate)], 1).reshape(D, MC, 1, 128)
    up = np.concatenate([columns(L0_cond_w_up), arr(L0_cond_sw_up)], 1).reshape(D, MC, 1, 128)
    w_down = np.concatenate([arr(L0_cond_w_down).reshape(E * M, D), arr(L0_cond_sw_down)], 0)
    eye = np.eye(128, dtype=np.float32)
    descending = np.broadcast_to(np.arange(E, 0, -1, dtype=np.float32), (128, E))
    b_of = np.eye(16, dtype=np.float32)
    diagonal = np.repeat(b_of, E, axis=1)
    expert_of = np.tile(np.repeat(np.eye(E, dtype=np.float32), M, axis=1), (2, 1))
    block_of = np.repeat(b_of, HID // NB, axis=1)
    last_row = np.zeros((NB + 2, 1), np.float32)
    last_row[-1] = -1
    arrays = {
        "x_t": arr(x).reshape(N_TOK, D).T,
        "w_in": np.concatenate([gate, up], 2).reshape(D, 2 * MC * 128),
        "w_down": w_down.reshape(MC, 128, D).transpose(1, 0, 2).reshape(128, MC * D),
        "w1_t": arr(L0_ffn_w1).T,
        "w2_t": arr(L0_ffn_w2).T.reshape(FC, 128, D).transpose(1, 0, 2).reshape(128, FC * D),
        "wt_t": np.concatenate([arr(L0_cond_wt).T, arr(L0_ffn_w_router)], 1),
        "wg_t": arr(L0_cond_wg).T,
        "cond_t": arr(cond_64).T,
        "b_router": arr(L0_ffn_b_router).reshape(1, NB),
        "b1": arr(L0_ffn_b1).reshape(1, HID),
        "b2": arr(L0_ffn_b2).reshape(D, 1),
        "const_rows": np.concatenate([eye, descending], 1),
        "const_sel": np.concatenate([last_row, np.pad(np.concatenate([diagonal, expert_of, block_of], 1),
                                                      ((0, 2), (0, 0)))], 1),
    }
    nc = bacc.Bacc("TRN2", target_bir_lowering=False, num_devices=1)
    arrays = {n: np.ascontiguousarray(a) for n, a in arrays.items()}
    args = [nc.dram_tensor(n, a.shape, mybir.dt.from_np(a.dtype), kind="ExternalInput").ap()
            for n, a in arrays.items()]
    args.append(nc.dram_tensor("out", (D, N_TOK), mybir.dt.float32, kind="ExternalOutput").ap())
    build(nc, *args)
    r = run_bass_kernel_spmd(nc, [arrays], core_ids=[0])
    return r.results[0]["out"].T.reshape(16, 128, 128)
```

```python
from contextlib import ExitStack

import concourse.bass as bass
from concourse import mybir

N_TOK, D, E, M, G, B = 2048, 128, 8, 64, 64, 16
HID, NB = 512, 16
TOKENS = 512
GROUPS = N_TOK // TOKENS
TILES = N_TOK // 128
TG = TOKENS // 128
EC = E * M // 128
MC = EC + 1
FC = HID // 128
TOP2 = 4
PAD = 8 - TOP2
PENALTY = -(2.0 ** 127)
TINY = 2.0 ** -126


IDENT, IOTA, WT, WR, B2, WG, COND, SMALL_COLS = (sum((128, E, E, NB, 1, E, B)[:i]) for i in range(8))
NEG, BR, DIAG, SEL_W, SEL_P, SEL_COLS = (sum((1, NB, B * E, EC * 128, HID)[:i]) for i in range(6))


def build(nc: bass.Bass, x_t, w_in, w_down, w1_t, w2_t, small, select, out):
    f32, f32r = mybir.dt.float32, mybir.dt.float32r
    ALU, ACT, AX = mybir.AluOpType, mybir.ActivationFunctionType, mybir.AxisListType

    ctx = ExitStack()
    with ctx:
        def sb(name, shape, dt=f32):
            return ctx.enter_context(nc.sbuf_tensor(name, shape, dt))

        def sem(name):
            return ctx.enter_context(nc.semaphore(name))

        x_raw = sb("x_raw", [128, N_TOK])
        win_raw = sb("win_raw", [128, 2 * MC * 128])
        wdn_raw = sb("wdn_raw", [128, MC * 128])
        w1_raw = sb("w1_raw", [128, HID])
        w2_raw = sb("w2_raw", [128, HID])
        small_sb = sb("small_sb", [128, SMALL_COLS])
        ident, iota = small_sb[:, IDENT:IOTA], small_sb[:, IOTA:WT]
        wt_sb, wr_sb, b2_sb = small_sb[:, WT:WR], small_sb[:, WR:B2], small_sb[:, B2:WG]
        wg_sb, cond_sb = small_sb[0:G, WG:COND], small_sb[0:G, COND:]
        sel_sb = sb("sel_sb", [NB + 2, SEL_COLS])
        x_hi, x_lo = sb("x_hi", [128, N_TOK], f32r), sb("x_lo", [128, N_TOK], f32r)
        win_hi, win_lo = sb("win_hi", [128, 2 * MC * 128], f32r), sb("win_lo", [128, 2 * MC * 128], f32r)
        wdn_hi, wdn_lo = sb("wdn_hi", [128, MC * 128], f32r), sb("wdn_lo", [128, MC * 128], f32r)
        w1_hi, w1_lo = sb("w1_hi", [128, HID], f32r), sb("w1_lo", [128, HID], f32r)
        w2_hi, w2_lo = sb("w2_hi", [128, HID], f32r), sb("w2_lo", [128, HID], f32r)
        wt_hl = sb("wt_hl", [128, 2 * E], f32r)
        wr_hl = sb("wr_hl", [128, 2 * NB], f32r)
        sel_w = sb("sel_w", [2 * E, EC * 128], f32r)
        sel_hi = sb("sel_hi", [NB + 2, HID], f32r)
        sel_p = sb("sel_p", [NB + 2, HID], f32r)
        w_tok = sb("w_tok", [128, TILES, 2 * E], f32r)
        w_row = sb("w_row", [2 * E, N_TOK], f32r)
        pen_row = sb("pen_row", [NB + 2, TOKENS], f32r)
        h_hi, h_lo = sb("h_hi", [128, MC, TOKENS], f32r), sb("h_lo", [128, MC, TOKENS], f32r)
        y_hi, y_lo = sb("y_hi", [128, TOKENS], f32r), sb("y_lo", [128, TOKENS], f32r)
        r_hi, r_lo = sb("r_hi", [128, FC, TOKENS], f32r), sb("r_lo", [128, FC, TOKENS], f32r)
        ones = sb("ones", [16, 128])
        bdiag = sb("bdiag", [B, B, E])
        gate = sb("gate", [128, MC, TOKENS])
        act_g = sb("act_g", [128, MC, TOKENS])
        gu = sb("gu", [128, EC, TOKENS])
        h = sb("h", [128, MC, TOKENS])
        y_out = sb("y_out", [128, N_TOK])
        mx1, z1, rank1, m2nd, rank2, den = (sb(n, [128, TILES]) for n in ("mx1", "z1", "rank1", "m2nd", "rank2", "den"))
        l1, d1, e1, v1, first, e1b, v2, v3, second, wun, wgt = (
            sb(n, [128, TILES, E]) for n in
            ("l1", "d1", "e1", "v1", "first", "e1b", "v2", "v3", "second", "wun", "wgt"))
        mx2, z2, rz2 = (sb(n, [128, TG]) for n in ("mx2", "z2", "rz2"))
        l2, d2, e2, s2 = (sb(n, [128, TG, NB]) for n in ("l2", "d2", "e2", "s2"))
        cand = sb("cand", [128, TG, NB + PAD])
        rest = sb("rest", [128, TG, NB + PAD])
        top8 = sb("top8", [128, TG, 8])
        pen = sb("pen", [128, TG, NB])

        bank = [ctx.enter_context(nc.psum_tensor(f"bank{i}", [128, TOKENS], f32)) for i in range(8)]
        g_bank, u_bank, w_bank, y_bank, o_bank = bank[0], bank[1:3], bank[3], bank[6], bank[7]
        turn_bank = bank[4]
        Z_BANKS = (5, 4, 5, 4)
        LAST_Z_BANKS = (0, 1, 2, 3)
        W_ROW_BANKS = (4, 4, 5, 7)

        def logits(b, first_tile, tiles, n):
            at = first_tile * 2 * n
            return bank[b][:, at:at + tiles * 2 * n].rearrange("p (t s e) -> p t s e", s=2, e=n)

        L1_BANKS = (5, 7)
        PART1 = (slice(0, TG), slice(TG, TILES))

        x_in = [sem(f"x_in{g}") for g in range(GROUPS)]
        win_in = [sem(f"win_in{c}") for c in range(3)]
        small_in, sel_in, wdn_in, w1_in, w2_in = (sem(n) for n in ("small_in", "sel_in", "wdn_in", "w1_in", "w2_in"))
        x_hi_ready, x0_lo_ready, x_lo_ready = sem("x_hi_ready"), sem("x0_lo_ready"), sem("x_lo_ready")
        w_hi_ready, w_lo_ready = sem("w_hi_ready"), sem("w_lo_ready")
        w_hi_ready2, w_lo_ready2 = sem("w_hi_ready2"), sem("w_lo_ready2")
        ones_ready, sel_w_ready, sel_hi_ready, sel_p_ready, pad_ready = (sem(n) for n in (
            "ones_ready", "sel_w_ready", "sel_hi_ready", "sel_p_ready", "pad_ready"))
        router_hi_ready, router_lo_ready = sem("router_hi_ready"), sem("router_lo_ready")
        lg_ready, bdiag_ready, logit1_ready, d1_ready, e1_ready = (sem(n) for n in (
            "lg_ready", "bdiag_ready", "logit1_ready", "d1_ready", "e1_ready"))
        w_tok_ready, w_turned, w_row_ready = sem("w_tok_ready"), sem("w_turned"), sem("w_row_ready")
        g_ready, u_ready, wb_ready, y_ready, z_ready, o_ready, logit2_ready, pen_turned = (sem(n) for n in (
            "g_ready", "u_ready", "wb_ready", "y_ready", "z_ready", "o_ready", "logit2_ready", "pen_turned"))
        gate_ready, h_hi_ready, y_hi_ready, r_hi_ready, e2_ready, pen_row_ready = (sem(n) for n in (
            "gate_ready", "h_hi_ready", "y_hi_ready", "r_hi_ready", "e2_ready", "pen_row_ready"))
        act_g_done, gu_done, h_done, y_lo_ready, r_lo_ready, out_done, d2_ready, pen_ready = (sem(n) for n in (
            "act_g_done", "gu_done", "h_done", "y_lo_ready", "r_lo_ready", "out_done", "d2_ready", "pen_ready"))
        h_lo_ready, step1, step2, stored = sem("h_lo_ready"), sem("step1"), sem("step2"), sem("stored")

        WIN = ((0, 1), (1, 2), (2, MC))
        LATER = ((wdn_raw, wdn_hi, wdn_lo, wdn_in), (w1_raw, w1_hi, w1_lo, w1_in), (w2_raw, w2_hi, w2_lo, w2_in))

        def piece(w, n):
            return w[:, WIN[n][0] * 256:WIN[n][1] * 256]

        def group(t, g):
            return t[:, bass.ts(g, TOKENS)]

        block = ctx.enter_context(nc.Block())

        @block.sync
        def _(sp):
            def load_x(g):
                sp.dma_start(group(x_raw, g), group(x_t, g)).then_inc(x_in[g], 16)

            def load_w(n):
                sp.dma_start(piece(win_raw, n), piece(w_in, n)).then_inc(win_in[n], 16)

            load_x(0)
            sp.dma_start(small_sb[:, :], small).then_inc(small_in, 16)
            load_w(0)
            sp.dma_start(sel_sb[:, :], select).then_inc(sel_in, 16)
            load_w(1)
            load_x(1)
            load_w(2)
            load_x(2)
            load_x(3)
            sp.dma_start(wdn_raw[:, :], w_down).then_inc(wdn_in, 16)
            sp.dma_start(w1_raw[:, :], w1_t).then_inc(w1_in, 16)
            sp.dma_start(w2_raw[:, :], w2_t).then_inc(w2_in, 16)
            with sp.Fori(0, GROUPS) as f:
                sp.wait_ge(out_done, f + 1)
                sp.dma_start(group(out, f), group(y_out, f)).then_inc(stored, 16)
            sp.wait_ge(stored, 16 * GROUPS)

        @block.gpsimd
        def _(pool):
            nc.gpsimd.memset(ones[:, :], 1.0).then_inc(ones_ready, 1)
            nc.gpsimd.memset(pen_row[:, :].bitcast(f32), 1.0).then_inc(ones_ready, 1)
            nc.gpsimd.memset(cand[:, :, NB:], -1.0).then_inc(pad_ready, 1)

            def x_low(g):
                pool.wait_ge(x_hi_ready, g + 1)
                nc.gpsimd.tensor_tensor(group(x_lo, g), group(x_raw, g), group(x_hi, g).bitcast(f32),
                                        ALU.subtract).then_inc(x_lo_ready, 1)

            def w_low(n):
                raw, hi, lo, _ = LATER[n]
                pool.wait_ge(w_hi_ready2, n + 1)
                nc.gpsimd.tensor_tensor(lo[:, :], raw[:, :], hi[:, :].bitcast(f32),
                                        ALU.subtract).then_inc(w_lo_ready2, 1)

            def h_low(g, c):
                pool.wait_ge(h_hi_ready, MC * g + c + 1)
                nc.gpsimd.tensor_tensor(h_lo[:, c, :], h[:, c, :], h_hi[:, c, :].bitcast(f32),
                                        ALU.subtract).then_inc(h_lo_ready, 1)

            x_low(1)
            x_low(2)
            x_low(3)
            h_low(0, 0)
            w_low(0)
            for c in range(1, MC):
                h_low(0, c)
            w_low(1)
            w_low(2)
            with pool.Fori(1, GROUPS) as g:
                for c in range(MC):
                    h_low(g, c)

        @block.scalar
        def _(act):
            def x_high(g):
                act.wait_ge(x_in[g], 16)
                nc.scalar.activation(group(x_hi, g), group(x_raw, g), ACT.Copy).then_inc(x_hi_ready, 1)

            def win_high(n):
                act.wait_ge(win_in[n], 16)
                nc.scalar.activation(piece(win_hi, n), piece(win_raw, n), ACT.Copy).then_inc(w_hi_ready, 1)

            def w_high(n):
                raw, hi, _, loaded = LATER[n]
                act.wait_ge(loaded, 16)
                nc.scalar.activation(hi[:, :], raw[:, :], ACT.Copy).then_inc(w_hi_ready2, 1)

            def exp1(part):
                act.wait_ge(d1_ready, part + 1)
                nc.scalar.activation(e1[:, PART1[part], :], d1[:, PART1[part], :], ACT.Exp,
                                     scale=0.5).then_inc(e1_ready, 1)

            def w_rows(g):
                act.wait_ge(w_turned, g + 1)
                nc.scalar.activation(group(w_row, g), bank[W_ROW_BANKS[g]][0:2 * E, :],
                                     ACT.Copy).then_inc(w_row_ready, 1)

            def gates(g, c):
                act.wait_ge(g_ready, MC * g + c + 1)
                nc.scalar.activation(gate[:, c, :], g_bank[:, :], ACT.Copy).then_inc(gate_ready, 1)

            def h_high(g, c):
                if c == EC:
                    act.wait_ge(gu_done, MC * (g + 1))
                else:
                    act.wait_ge(h_done, EC * g + c + 1)
                nc.scalar.activation(h_hi[:, c, :], h[:, c, :], ACT.Copy).then_inc(h_hi_ready, 1)

            def y_high(g):
                act.wait_ge(y_ready, g + 1)
                nc.scalar.activation(y_hi[:, :], y_bank[:, :], ACT.Copy).then_inc(y_hi_ready, 1)

            def exp2(g):
                act.wait_ge(d2_ready, g + 1)
                nc.scalar.activation(e2[:, :, :], d2[:, :, :], ACT.Exp).then_inc(e2_ready, 1)

            def pen_rows(f):
                act.wait_ge(pen_turned, f + 1)
                nc.scalar.activation(pen_row[0:NB, :], turn_bank[0:NB, :], ACT.Copy).then_inc(pen_row_ready, 1)

            def relus(f, c, banks=Z_BANKS):
                act.wait_ge(z_ready, FC * f + c + 1)
                nc.scalar.activation(r_hi[:, c, :], bank[banks[c]][:, :], ACT.Relu).then_inc(r_hi_ready, 1)

            def body(g, experts=True, ffn=True):
                h_high(g - 1, EC)
                if experts:
                    gates(g, 0)
                if ffn:
                    pen_rows(g - 2)
                if experts:
                    h_high(g, 0)
                if ffn:
                    relus(g - 2, 0)
                    relus(g - 2, 1)
                if experts:
                    gates(g, 1)
                if ffn:
                    relus(g - 2, 2)
                    relus(g - 2, 3)
                y_high(g - 1)
                if experts:
                    h_high(g, 1)
                    gates(g, 2)
                    h_high(g, 2)
                exp2(g - 1)
                if experts:
                    gates(g, 3)
                    h_high(g, 3)
                    gates(g, 4)

            x_high(0)
            act.wait_ge(small_in, 16)
            nc.scalar.activation(wt_hl[:, 0:E], wt_sb, ACT.Copy).then_inc(router_hi_ready, 1)
            nc.scalar.activation(wr_hl[:, 0:NB], wr_sb, ACT.Copy).then_inc(router_hi_ready, 1)
            win_high(0)
            win_high(1)
            x_high(1)
            exp1(0)
            act.wait_ge(sel_in, 16)
            nc.scalar.activation(sel_w[:, :], sel_sb[0:2 * E, SEL_W:SEL_P], ACT.Copy).then_inc(sel_w_ready, 1)
            x_high(2)
            x_high(3)
            gates(0, 0)
            win_high(2)
            gates(0, 1)
            w_rows(0)
            nc.scalar.activation(sel_hi[:, :], sel_sb[:, SEL_P:], ACT.Copy).then_inc(sel_hi_ready, 1)
            w_high(0)
            h_high(0, 0)
            exp1(1)
            gates(0, 2)
            h_high(0, 1)
            gates(0, 3)
            h_high(0, 2)
            gates(0, 4)
            h_high(0, 3)
            act.wait_ge(ones_ready, 2)
            for g in range(1, GROUPS):
                w_rows(g)
            w_high(1)
            w_high(2)
            body(1, ffn=False)
            with act.Fori(2, GROUPS) as g:
                body(g)
            body(GROUPS, experts=False)
            pen_rows(GROUPS - 1)
            for c in range(FC):
                relus(GROUPS - 1, c, LAST_Z_BANKS)

        @block.vector
        def _(dve):
            v = nc.vector

            def win_low(n):
                dve.wait_ge(w_hi_ready, n + 1)
                v.tensor_tensor(piece(win_lo, n), piece(win_raw, n), piece(win_hi, n).bitcast(f32),
                                ALU.subtract).then_inc(w_lo_ready, 1)

            def spread(t, n):
                return t.unsqueeze(2).to_broadcast([128, t.shape[1], n])

            STEPS1 = 18

            def route(part, n):
                ts = PART1[part]
                tiles = ts.stop - ts.start
                count = iota.unsqueeze(1).to_broadcast([128, tiles, E])

                def after(step):
                    dve.wait_ge(step1, STEPS1 * part + step)

                if n == 0:
                    dve.wait_ge(logit1_ready, part + 1)
                    v.reduce_sum(l1[:, ts, :], logits(L1_BANKS[part], 0, tiles, E).rearrange("p t s e -> p t e s"),
                                 AX.X).then_inc(step1, 1)
                elif n == 1:
                    after(1)
                    v.reduce_max(mx1[:, ts], l1[:, ts, :], AX.X).then_inc(step1, 1)
                elif n == 2:
                    after(2)
                    v.tensor_tensor(d1[:, ts, :], l1[:, ts, :], spread(mx1[:, ts], E), ALU.subtract)\
                        .then_inc(d1_ready, 1)
                elif n == 3:
                    dve.wait_ge(d1_ready, part + 1)
                    v.scalar_tensor_tensor(v1[:, ts, :], d1[:, ts, :], 0.0, count, ALU.is_ge, ALU.mult)\
                        .then_inc(step1, 1)
                elif n == 4:
                    after(3)
                    v.reduce_max(rank1[:, ts], v1[:, ts, :], AX.X).then_inc(step1, 1)
                elif n == 5:
                    after(4)
                    v.tensor_tensor(first[:, ts, :], v1[:, ts, :], spread(rank1[:, ts], E), ALU.is_equal)\
                        .then_inc(step1, 1)
                elif n == 6:
                    dve.wait_ge(e1_ready, part + 1)
                    v.reduce_sum(z1[:, ts], e1[:, ts, :], AX.X).then_inc(step1, 1)
                elif n == 7:
                    after(5)
                    v.scalar_tensor_tensor(e1b[:, ts, :], first[:, ts, :], -2.0, e1[:, ts, :], ALU.mult, ALU.add)\
                        .then_inc(step1, 1)
                elif n == 8:
                    after(7)
                    v.reduce_max(m2nd[:, ts], e1b[:, ts, :], AX.X).then_inc(step1, 1)
                elif n == 9:
                    after(8)
                    v.tensor_tensor(v2[:, ts, :], e1b[:, ts, :], spread(m2nd[:, ts], E), ALU.is_equal)\
                        .then_inc(step1, 1)
                elif n == 10:
                    v.scalar_tensor_tensor(den[:, ts], z1[:, ts], 1e-20, m2nd[:, ts], ALU.mult, ALU.add)\
                        .then_inc(step1, 1)
                elif n == 11:
                    after(9)
                    v.tensor_tensor(v3[:, ts, :], v2[:, ts, :], count, ALU.mult).then_inc(step1, 1)
                elif n == 12:
                    after(10)
                    v.tensor_scalar(den[:, ts], den[:, ts], 1.0, None, ALU.add).then_inc(step1, 1)
                elif n == 13:
                    after(11)
                    v.reduce_max(rank2[:, ts], v3[:, ts, :], AX.X).then_inc(step1, 1)
                elif n == 14:
                    after(12)
                    v.reciprocal(den[:, ts], den[:, ts]).then_inc(step1, 1)
                elif n == 15:
                    after(13)
                    v.tensor_tensor(second[:, ts, :], v3[:, ts, :], spread(rank2[:, ts], E), ALU.is_equal)\
                        .then_inc(step1, 1)
                elif n == 16:
                    after(15)
                    v.tensor_tensor(second[:, ts, :], second[:, ts, :], spread(m2nd[:, ts], E), ALU.mult)\
                        .then_inc(step1, 1)
                elif n == 17:
                    after(16)
                    v.tensor_tensor(wun[:, ts, :], second[:, ts, :], first[:, ts, :], ALU.add).then_inc(step1, 1)
                elif n == 18:
                    after(17)
                    v.tensor_tensor(wgt[:, ts, :], wun[:, ts, :], spread(den[:, ts], E), ALU.mult)\
                        .then_inc(step1, 1)
                elif n == 19:
                    after(18)
                    v.tensor_copy(w_tok[:, ts, 0:E], wgt[:, ts, :]).then_inc(w_tok_ready, 1)
                elif n == 20:
                    dve.wait_ge(w_tok_ready, 2 * part + 1)
                    v.tensor_tensor(w_tok[:, ts, E:], wgt[:, ts, :], w_tok[:, ts, 0:E].bitcast(f32),
                                    ALU.subtract).then_inc(w_tok_ready, 1)

            def leaky(g, c):
                dve.wait_ge(gate_ready, MC * g + c + 1)
                v.scalar_tensor_tensor(act_g[:, c, :], gate[:, c, :], 0.01, gate[:, c, :],
                                       ALU.mult, ALU.max).then_inc(act_g_done, 1)

            def times_up(g, c):
                dve.wait_ge(u_ready, MC * g + c + 1)
                dve.wait_ge(act_g_done, MC * g + c + 1)
                v.tensor_tensor(h[:, c, :] if c == EC else gu[:, c, :], u_bank[c % 2][:, :],
                                act_g[:, c, :], ALU.mult).then_inc(gu_done, 1)

            def times_weight(g, c):
                dve.wait_ge(wb_ready, EC * g + c + 1)
                dve.wait_ge(gu_done, MC * g + c + 1)
                v.tensor_tensor(h[:, c, :], w_bank[:, :], gu[:, c, :], ALU.mult).then_inc(h_done, 1)

            def y_low(g):
                dve.wait_ge(y_hi_ready, g + 1)
                v.tensor_tensor(y_lo[:, :], y_bank[:, :], y_hi[:, :].bitcast(f32),
                                ALU.subtract).then_inc(y_lo_ready, 1)

            def relu_low(f, c, banks=Z_BANKS):
                dve.wait_ge(r_hi_ready, FC * f + c + 1)
                v.scalar_tensor_tensor(r_lo[:, c, :], bank[banks[c]][:, :], 0.0, r_hi[:, c, :].bitcast(f32),
                                       ALU.max, ALU.subtract).then_inc(r_lo_ready, 1)

            def result(f):
                dve.wait_ge(o_ready, f + 1)
                v.scalar_tensor_tensor(group(y_out, f), o_bank[:, :], b2_sb, group(x_raw, f),
                                       ALU.add, ALU.add).then_inc(out_done, 1)

            STEPS2 = 9

            def before_max(g):
                dve.wait_ge(step2, STEPS2 * g + 6)

            def before_replace(g):
                dve.wait_ge(step2, STEPS2 * g + 8)

            def pick(g, n):
                if n == 0:
                    dve.wait_ge(logit2_ready, g + 1)
                    v.reduce_sum(l2[:, :, :], logits(4, 0, TG, NB).rearrange("p t s e -> p t e s"), AX.X)\
                        .then_inc(step2, 1)
                elif n == 1:
                    dve.wait_ge(step2, STEPS2 * g + 1)
                    v.reduce_max(mx2[:, :], l2[:, :, :], AX.X).then_inc(step2, 1)
                elif n == 2:
                    dve.wait_ge(step2, STEPS2 * g + 2)
                    v.tensor_tensor(d2[:, :, :], l2[:, :, :], spread(mx2[:, :], NB), ALU.subtract)\
                        .then_inc(d2_ready, 1)
                elif n == 3:
                    dve.wait_ge(e2_ready, g + 1)
                    v.reduce_sum(z2[:, :], e2[:, :, :], AX.X).then_inc(step2, 1)
                elif n == 4:
                    dve.wait_ge(step2, STEPS2 * g + 3)
                    v.reciprocal(rz2[:, :], z2[:, :]).then_inc(step2, 1)
                elif n == 5:
                    dve.wait_ge(step2, STEPS2 * g + 4)
                    v.tensor_tensor(s2[:, :, :], e2[:, :, :], spread(rz2[:, :], NB), ALU.mult).then_inc(step2, 1)
                elif n == 6:
                    dve.wait_ge(step2, STEPS2 * g + 5)
                    v.scalar_tensor_tensor(cand[:, :, 0:NB], s2[:, :, :], TINY, s2[:, :, :],
                                           ALU.is_ge, ALU.mult).then_inc(step2, 1)
                elif n == 7:
                    for t in range(TG):
                        last = v.max(top8[:, t, :], cand[:, t, 0:NB])
                    last.then_inc(step2, 1)
                elif n == 8:
                    dve.wait_ge(step2, STEPS2 * g + 7)
                    v.memset(top8[:, :, TOP2:], -1.0).then_inc(step2, 1)
                elif n == 9:
                    for t in range(TG):
                        last = v.match_replace(rest[:, t, :], top8[:, t, :], cand[:, t, :], 2.0)
                    last.then_inc(step2, 1)
                elif n == 10:
                    dve.wait_ge(step2, STEPS2 * g + 9)
                    v.tensor_scalar(pen[:, :, :], rest[:, :, 0:NB], 2.0, PENALTY,
                                    ALU.is_lt, ALU.mult).then_inc(pen_ready, 1)

            def chunk(g, c):
                leaky(g, c)
                times_up(g, c)
                if c < EC:
                    times_weight(g, c)

            def body(g, ffn=True):
                if ffn:
                    chunk(g, 0)
                    relu_low(g - 2, 0)
                    relu_low(g - 2, 1)
                    chunk(g, 1)
                    relu_low(g - 2, 2)
                    relu_low(g - 2, 3)
                else:
                    chunk(g, 0)
                    chunk(g, 1)
                y_low(g - 1)
                chunk(g, 2)
                pick(g - 1, 0)
                pick(g - 1, 1)
                pick(g - 1, 2)
                leaky(g, 3)
                pick(g - 1, 3)
                times_up(g, 3)
                pick(g - 1, 4)
                pick(g - 1, 5)
                times_weight(g, 3)
                pick(g - 1, 6)
                if ffn:
                    before_max(g - 1)
                    result(g - 2)
                pick(g - 1, 7)
                pick(g - 1, 8)
                before_replace(g - 1)
                leaky(g, 4)
                pick(g - 1, 9)
                times_up(g, 4)
                pick(g - 1, 10)

            dve.wait_ge(router_hi_ready, 2)
            v.tensor_tensor(wt_hl[:, E:], wt_sb, wt_hl[:, 0:E].bitcast(f32), ALU.subtract)
            v.tensor_tensor(wr_hl[:, NB:], wr_sb, wr_hl[:, 0:NB].bitcast(f32),
                            ALU.subtract).then_inc(router_lo_ready, 1)
            dve.wait_ge(x_hi_ready, 1)
            v.tensor_tensor(group(x_lo, 0), group(x_raw, 0), group(x_hi, 0).bitcast(f32),
                            ALU.subtract).then_inc(x0_lo_ready, 1)
            win_low(0)
            dve.wait_ge(sel_in, 16)
            dve.wait_ge(lg_ready, 1)
            v.tensor_tensor(bdiag[:, :, :], o_bank[0:B, 0:E].unsqueeze(1).to_broadcast([B, B, E]),
                            sel_sb[0:B, DIAG:SEL_W].rearrange("p (t e) -> p t e", e=E),
                            ALU.mult).then_inc(bdiag_ready, 1)
            for n in range(7):
                route(0, n)
            win_low(1)
            for n in range(7, 21):
                route(0, n)
            leaky(0, 0)
            times_up(0, 0)
            leaky(0, 1)
            times_weight(0, 0)
            times_up(0, 1)
            win_low(2)
            route(1, 0)
            times_weight(0, 1)
            route(1, 1)
            route(1, 2)
            route(1, 3)
            leaky(0, 2)
            route(1, 4)
            times_up(0, 2)
            route(1, 5)
            route(1, 6)
            times_weight(0, 2)
            route(1, 7)
            leaky(0, 3)
            route(1, 8)
            times_up(0, 3)
            route(1, 9)
            route(1, 10)
            times_weight(0, 3)
            route(1, 11)
            route(1, 12)
            leaky(0, 4)
            route(1, 13)
            route(1, 14)
            times_up(0, 4)
            for n in range(15, 21):
                route(1, n)
            dve.wait_ge(sel_hi_ready, 1)
            v.scalar_tensor_tensor(sel_p[:, :], sel_hi[:, :].bitcast(f32), sel_sb[:, NEG:BR], sel_sb[:, SEL_P:],
                                   ALU.mult, ALU.add).then_inc(sel_p_ready, 1)
            dve.wait_ge(pad_ready, 1)
            body_1 = 1
            chunk(body_1, 0)
            chunk(body_1, 1)
            y_low(0)
            chunk(body_1, 2)
            for n in range(3):
                pick(0, n)
            leaky(body_1, 3)
            pick(0, 3)
            times_up(body_1, 3)
            pick(0, 4)
            pick(0, 5)
            times_weight(body_1, 3)
            pick(0, 6)
            before_max(0)
            pick(0, 7)
            pick(0, 8)
            before_replace(0)
            leaky(body_1, 4)
            pick(0, 9)
            times_up(body_1, 4)
            pick(0, 10)
            with dve.Fori(2, GROUPS) as g:
                body(g)
            last_g = GROUPS - 1
            for c in range(FC):
                relu_low(last_g - 1, c)
            y_low(last_g)
            for n in range(7):
                pick(last_g, n)
            before_max(last_g)
            pick(last_g, 7)
            pick(last_g, 8)
            before_replace(last_g)
            pick(last_g, 9)
            pick(last_g, 10)
            result(last_g - 1)
            for c in range(FC):
                relu_low(last_g, c, LAST_Z_BANKS)
            result(last_g)

        @block.tensor
        def _(pe):
            def product(dst, w_hi, w_lo, m_hi, m_lo, start, stop):
                nc.tensor.matmul(dst, w_hi, m_hi, start=start, stop=False)
                nc.tensor.matmul(dst, w_lo, m_hi, start=False, stop=False)
                return nc.tensor.matmul(dst, w_hi, m_lo, start=False, stop=stop)

            def tile_logits(b, n, place, tile, hi, lo, w_hl):
                at = slice(tile * 128, (tile + 1) * 128)
                to = place * 2 * n
                nc.tensor.matmul(bank[b][:, to:to + 2 * n], hi[:, at], w_hl[:, :],
                                 start=(place == 0), stop=False, skip_group_check=True)
                nc.tensor.matmul(bank[b][:, to:to + n], lo[:, at], w_hl[:, 0:n],
                                 start=False, stop=False, skip_group_check=True)

            def route(part):
                ts = PART1[part]
                for t in range(ts.start, ts.stop):
                    if t % TG == 0:
                        pe.wait_ge(x_hi_ready, t // TG + 1)
                        if t:
                            pe.wait_ge(x_lo_ready, t // TG)
                        else:
                            pe.wait_ge(x0_lo_ready, 1)
                    tile_logits(L1_BANKS[part], E, t - ts.start, t, x_hi, x_lo, wt_hl)
                if part == 0:
                    pe.wait_ge(bdiag_ready, 1)
                nc.tensor.matmul(logits(L1_BANKS[part], 0, ts.stop - ts.start, E)[:, :, 0, :], ones[:, :],
                                 bdiag[:, ts, :], start=False, stop=True,
                                 skip_group_check=True).then_inc(logit1_ready, 1)

            def turn_weights(g):
                for t in range(TG):
                    last = nc.tensor.transpose(bank[W_ROW_BANKS[g]][0:2 * E, t * 128:(t + 1) * 128],
                                               w_tok[:, g * TG + t, :].bitcast(f32), ident)
                last.then_inc(w_turned, 1)

            def weights_in(c, up):
                at = (2 * c + up) * 128
                return win_hi[:, at:at + 128], win_lo[:, at:at + 128]

            def gate_up(g, c, first=False):
                if not first:
                    pe.wait_ge(gate_ready, MC * g + c)
                product(g_bank[:, :], *weights_in(c, 0), group(x_hi, g), group(x_lo, g),
                        True, True).then_inc(g_ready, 1)
                if c >= 2:
                    pe.wait_ge(gu_done, MC * g + c - 1)
                elif c == 0 and not first:
                    pe.wait_ge(gu_done, MC * g)
                product(u_bank[c % 2][:, :], *weights_in(c, 1), group(x_hi, g), group(x_lo, g),
                        True, True).then_inc(u_ready, 1)

            def weight_bank(g, c):
                nc.tensor.matmul(w_bank[:, :], sel_w[:, c * 128:(c + 1) * 128], group(w_row, g),
                                 start=True, stop=True).then_inc(wb_ready, 1)

            def gate_up_weight(g, c):
                if c >= 1:
                    pe.wait_ge(gate_ready, MC * g + c)
                    product(g_bank[:, :], *weights_in(c, 0), group(x_hi, g), group(x_lo, g),
                            True, True).then_inc(g_ready, 1)
                    pe.wait_ge(h_done, EC * g + c)
                    product(u_bank[c % 2][:, :], *weights_in(c, 1), group(x_hi, g), group(x_lo, g),
                            True, True).then_inc(u_ready, 1)
                else:
                    gate_up(g, c)
                if c < EC:
                    weight_bank(g, c)

            def down(g, c):
                at = slice(c * 128, (c + 1) * 128)
                pe.wait_ge(h_hi_ready, MC * g + c + 1)
                pe.wait_ge(h_lo_ready, MC * g + c + 1)
                last = product(y_bank[:, :], wdn_hi[:, at], wdn_lo[:, at], h_hi[:, c, :], h_lo[:, c, :],
                               c == 0, c == MC - 1)
                if c == MC - 1:
                    last.then_inc(y_ready, 1)

            def router2(g):
                pe.wait_ge(y_hi_ready, g + 1)
                pe.wait_ge(y_lo_ready, g + 1)
                for t in range(TG):
                    tile_logits(4, NB, t, t, y_hi, y_lo, wr_hl)
                nc.tensor.matmul(logits(4, 0, TG, NB)[:, :, 0, :], ones[0:1, :],
                                 sel_sb[0:1, BR:DIAG].unsqueeze(1).to_broadcast([1, TG, NB]),
                                 start=False, stop=True, skip_group_check=True).then_inc(logit2_ready, 1)

            def turn_penalties(f):
                pe.wait_ge(pen_ready, f + 1)
                for t in range(TG):
                    last = nc.tensor.transpose(turn_bank[0:NB, t * 128:(t + 1) * 128], pen[:, t, :], ident)
                last.then_inc(pen_turned, 1)

            def ffn_up(c, banks=Z_BANKS):
                at = slice(c * 128, (c + 1) * 128)
                product(bank[banks[c]][:, :], w1_hi[:, at], w1_lo[:, at], y_hi[:, :], y_lo[:, :], True, False)

            def penalise(c, banks=Z_BANKS):
                nc.tensor.matmul(bank[banks[c]][:, :], sel_p[:, c * 128:(c + 1) * 128], pen_row[:, :],
                                 start=False, stop=True).then_inc(z_ready, 1)

            def ffn_down(f, c):
                at = slice(c * 128, (c + 1) * 128)
                pe.wait_ge(r_hi_ready, FC * f + c + 1)
                pe.wait_ge(r_lo_ready, FC * f + c + 1)
                last = product(o_bank[:, :], w2_hi[:, at], w2_lo[:, at], r_hi[:, c, :], r_lo[:, c, :],
                               c == 0, c == FC - 1)
                if c == FC - 1:
                    last.then_inc(o_ready, 1)

            def body(g, experts=True, ffn=True):
                f = g - 2
                if experts:
                    gate_up_weight(g, 0)
                down(g - 1, 3)
                if ffn:
                    turn_penalties(f)
                    ffn_up(0)
                    pe.wait_ge(pen_row_ready, f + 1)
                    penalise(0)
                    ffn_up(1)
                    penalise(1)
                if experts:
                    gate_up_weight(g, 1)
                if ffn:
                    for c in (2, 3):
                        pe.wait_ge(r_lo_ready, FC * f + c - 1)
                        ffn_up(c)
                        penalise(c)
                down(g - 1, 4)
                if experts:
                    gate_up_weight(g, 2)
                if ffn:
                    ffn_down(f, 0)
                    ffn_down(f, 1)
                router2(g - 1)
                if experts:
                    gate_up_weight(g, 3)
                    down(g, 0)
                if ffn:
                    ffn_down(f, 2)
                    ffn_down(f, 3)
                if experts:
                    gate_up_weight(g, 4)
                    down(g, 1)
                    down(g, 2)

            pe.wait_ge(small_in, 16)
            nc.tensor.matmul(o_bank[0:B, 0:E], cond_sb, wg_sb, start=True, stop=True).then_inc(lg_ready, 1)
            pe.wait_ge(router_lo_ready, 1)
            pe.wait_ge(ones_ready, 1)
            route(0)
            pe.wait_ge(w_lo_ready, 1)
            gate_up(0, 0, first=True)
            pe.wait_ge(w_lo_ready, 2)
            pe.wait_ge(gate_ready, 1)
            product(g_bank[:, :], *weights_in(1, 0), group(x_hi, 0), group(x_lo, 0), True, True).then_inc(g_ready, 1)
            product(u_bank[1][:, :], *weights_in(1, 1), group(x_hi, 0), group(x_lo, 0), True, True).then_inc(u_ready, 1)
            route(1)
            pe.wait_ge(w_tok_ready, 2)
            turn_weights(0)
            pe.wait_ge(w_row_ready, 1)
            pe.wait_ge(sel_w_ready, 1)
            weight_bank(0, 0)
            pe.wait_ge(h_done, 1)
            weight_bank(0, 1)
            pe.wait_ge(w_lo_ready, 3)
            gate_up_weight(0, 2)
            gate_up_weight(0, 3)
            pe.wait_ge(w_lo_ready2, 1)
            down(0, 0)
            gate_up_weight(0, 4)
            down(0, 1)
            down(0, 2)
            pe.wait_ge(w_tok_ready, 4)
            for g in range(1, GROUPS):
                turn_weights(g)
            pe.wait_ge(w_row_ready, GROUPS)
            body(1, ffn=False)
            pe.wait_ge(sel_p_ready, 1)
            pe.wait_ge(w_lo_ready2, 3)
            with pe.Fori(2, GROUPS) as g:
                body(g)
            body(GROUPS, experts=False)
            f = GROUPS - 1
            for c in range(FC):
                ffn_up(c, LAST_Z_BANKS)
            turn_penalties(f)
            pe.wait_ge(pen_row_ready, f + 1)
            for c in range(FC):
                penalise(c, LAST_Z_BANKS)
            pe.wait_ge(out_done, f)
            for c in range(FC):
                ffn_down(f, c)


def kernel(x, cond_64, L0_cond_wt, L0_cond_wg, L0_cond_w_gate, L0_cond_w_up, L0_cond_w_down, L0_cond_sw_gate,
           L0_cond_sw_up, L0_cond_sw_down, L0_ffn_w_router, L0_ffn_b_router, L0_ffn_w1, L0_ffn_b1, L0_ffn_w2,
           L0_ffn_b2):
    import numpy as np
    import concourse.bacc as bacc
    from concourse.bass_utils import run_bass_kernel_spmd

    def arr(a):
        return np.asarray(a)

    def columns(w):
        return arr(w).transpose(1, 0, 2).reshape(D, E * M)

    def rows(a, n):
        return np.pad(a, ((0, n - a.shape[0]), (0, 0)))

    gate = np.concatenate([columns(L0_cond_w_gate), arr(L0_cond_sw_gate)], 1).reshape(D, MC, 1, 128)
    up = np.concatenate([columns(L0_cond_w_up), arr(L0_cond_sw_up)], 1).reshape(D, MC, 1, 128)
    w_down = np.concatenate([arr(L0_cond_w_down).reshape(E * M, D), arr(L0_cond_sw_down)], 0)
    identity = np.eye(128, dtype=np.float32)
    descending = np.broadcast_to(np.arange(E, 0, -1, dtype=np.float32), (128, E))
    minus_last = np.zeros((NB + 2, 1), np.float32)
    minus_last[-1] = -1
    diagonal = np.repeat(np.eye(B, dtype=np.float32), E, axis=1)
    expert_of = np.tile(np.repeat(np.eye(E, dtype=np.float32), M, axis=1), (2, 1))
    block_of = np.repeat(np.eye(NB, dtype=np.float32), HID // NB, axis=1)
    b1 = arr(L0_ffn_b1).reshape(1, HID)
    arrays = {
        "x_t": arr(x).reshape(N_TOK, D).T,
        "w_in": np.concatenate([gate, up], 2).reshape(D, 2 * MC * 128),
        "w_down": w_down.reshape(MC, 128, D).transpose(1, 0, 2).reshape(128, MC * D),
        "w1_t": arr(L0_ffn_w1).T,
        "w2_t": arr(L0_ffn_w2).T.reshape(FC, 128, D).transpose(1, 0, 2).reshape(128, FC * D),
        "small": np.concatenate([identity, descending, arr(L0_cond_wt).T, arr(L0_ffn_w_router),
                                 arr(L0_ffn_b2).reshape(D, 1), rows(arr(L0_cond_wg).T, 128),
                                 rows(arr(cond_64).T, 128)], 1),
        "select": np.concatenate([minus_last, rows(arr(L0_ffn_b_router).reshape(1, NB), NB + 2),
                                  rows(diagonal, NB + 2), rows(expert_of, NB + 2),
                                  np.concatenate([block_of, b1, b1], 0)], 1),
    }
    nc = bacc.Bacc("TRN2", target_bir_lowering=False, num_devices=1)
    arrays = {n: np.ascontiguousarray(a) for n, a in arrays.items()}
    args = [nc.dram_tensor(n, a.shape, mybir.dt.from_np(a.dtype), kind="ExternalInput").ap()
            for n, a in arrays.items()]
    args.append(nc.dram_tensor("out", (D, N_TOK), mybir.dt.float32, kind="ExternalOutput").ap())
    build(nc, *args)
    r = run_bass_kernel_spmd(nc, [arrays], core_ids=[0])
    return r.results[0]["out"].T.reshape(16, 128, 128)
```

```python
from contextlib import ExitStack

import concourse.bass as bass
from concourse import mybir

N_TOK, D, E, M, G, B = 2048, 128, 8, 64, 64, 16
HID, NB = 512, 16
TOKENS = 512
GROUPS = N_TOK // TOKENS
TILES = N_TOK // 128
TG = TOKENS // 128
EC = E * M // 128
MC = EC + 1
FC = HID // 128
TOP2 = 4
PAD = 8 - TOP2
PENALTY = -(2.0 ** 127)
TINY = 2.0 ** -126


IDENT, IOTA, WT, WR, B2, WG, COND, SMALL_COLS = (sum((128, E, E, NB, 1, E, B)[:i]) for i in range(8))
NEG, BR, DIAG, SEL_W, SEL_P, SEL_COLS = (sum((1, NB, B * E, EC * 128, HID)[:i]) for i in range(6))


def build(nc: bass.Bass, x_t, w_in, w_down, w1_t, w2_t, small, select, out):
    f32, f32r = mybir.dt.float32, mybir.dt.float32r
    ALU, ACT, AX = mybir.AluOpType, mybir.ActivationFunctionType, mybir.AxisListType

    ctx = ExitStack()
    with ctx:
        def sb(name, shape, dt=f32):
            return ctx.enter_context(nc.sbuf_tensor(name, shape, dt))

        def sem(name):
            return ctx.enter_context(nc.semaphore(name))

        x_raw = sb("x_raw", [128, N_TOK])
        win_raw = sb("win_raw", [128, 2 * MC * 128])
        wdn_raw = sb("wdn_raw", [128, MC * 128])
        w1_raw = sb("w1_raw", [128, HID])
        w2_raw = sb("w2_raw", [128, HID])
        small_sb = sb("small_sb", [128, SMALL_COLS])
        ident, iota = small_sb[:, IDENT:IOTA], small_sb[:, IOTA:WT]
        wt_sb, wr_sb, b2_sb = small_sb[:, WT:WR], small_sb[:, WR:B2], small_sb[:, B2:WG]
        wg_sb, cond_sb = small_sb[0:G, WG:COND], small_sb[0:G, COND:]
        sel_sb = sb("sel_sb", [NB + 2, SEL_COLS])
        x_hi, x_lo = sb("x_hi", [128, N_TOK], f32r), sb("x_lo", [128, N_TOK], f32r)
        win_hi, win_lo = sb("win_hi", [128, 2 * MC * 128], f32r), sb("win_lo", [128, 2 * MC * 128], f32r)
        wdn_hi, wdn_lo = sb("wdn_hi", [128, MC * 128], f32r), sb("wdn_lo", [128, MC * 128], f32r)
        w1_hi, w1_lo = sb("w1_hi", [128, HID], f32r), sb("w1_lo", [128, HID], f32r)
        w2_hi, w2_lo = sb("w2_hi", [128, HID], f32r), sb("w2_lo", [128, HID], f32r)
        wt_hl = sb("wt_hl", [128, 2 * E], f32r)
        wr_hl = sb("wr_hl", [128, 2 * NB], f32r)
        sel_w = sb("sel_w", [2 * E, EC * 128], f32r)
        sel_hi = sb("sel_hi", [NB + 2, HID], f32r)
        sel_p = sb("sel_p", [NB + 2, HID], f32r)
        w_tok = sb("w_tok", [128, TILES, 2 * E], f32r)
        w_row = sb("w_row", [2 * E, N_TOK], f32r)
        pen_row = sb("pen_row", [NB + 2, TOKENS], f32r)
        h_hi, h_lo = sb("h_hi", [128, MC, TOKENS], f32r), sb("h_lo", [128, MC, TOKENS], f32r)
        Y, Y_LAST = ((sb(f"{n}_hi", [128, TOKENS], f32r), sb(f"{n}_lo", [128, TOKENS], f32r)) for n in ("y", "y_last"))
        r_hi, r_lo = sb("r_hi", [128, FC, TOKENS], f32r), sb("r_lo", [128, FC, TOKENS], f32r)
        ones = sb("ones", [16, 128])
        bdiag = sb("bdiag", [B, B, E])
        gate = sb("gate", [128, MC, TOKENS])
        act_g = sb("act_g", [128, MC, TOKENS])
        gu = sb("gu", [128, EC, TOKENS])
        h = sb("h", [128, MC, TOKENS])
        y_out = sb("y_out", [128, N_TOK])
        mx1, z1, rank1, m2nd, rank2, den = (sb(n, [128, TILES]) for n in ("mx1", "z1", "rank1", "m2nd", "rank2", "den"))
        l1, d1, e1, v1, first, e1b, v2, v3, second, wun, wgt = (
            sb(n, [128, TILES, E]) for n in
            ("l1", "d1", "e1", "v1", "first", "e1b", "v2", "v3", "second", "wun", "wgt"))
        mx2, z2, rz2 = (sb(n, [128, TG]) for n in ("mx2", "z2", "rz2"))
        l2, d2, e2, s2 = (sb(n, [128, TG, NB]) for n in ("l2", "d2", "e2", "s2"))
        cand = sb("cand", [128, TG, NB + PAD])
        rest = sb("rest", [128, TG, NB + PAD])
        top8 = sb("top8", [128, TG, 8])
        pen = sb("pen", [128, TG, NB])

        bank = [ctx.enter_context(nc.psum_tensor(f"bank{i}", [128, TOKENS], f32)) for i in range(8)]
        y_bank, o_bank = bank[6], bank[7]
        turn_bank = bank[4]
        G_BANKS, G_BANKS_0, G_BANKS_1 = (0,) * MC, (0, 7, 0, 7, 0), (7, 0, 7, 0, 7)
        U_BANKS, U_BANKS_0 = (1, 2, 1, 2, 5), (1, 2, 5, 1, 2)
        W_BANKS, W_BANKS_0, W_BANKS_1 = (3,) * EC, (3, 4, 3, 4), (3, 4, 3, 4)
        Z_BANKS, Z_BANKS_4, Z_BANKS_5 = (5, 4, 5, 4), (1, 2, 0, 5), (3, 1, 2, 0)
        W_ROW_BANKS = (4, 5, 5, 5)

        def logits(b, first_tile, tiles, n):
            at = first_tile * 2 * n
            return bank[b][:, at:at + tiles * 2 * n].rearrange("p (t s e) -> p t s e", s=2, e=n)

        L1_BANKS = (5, 6)
        PART1 = (slice(0, TG), slice(TG, TILES))
        STEPS1 = 18

        x_in = [sem(f"x_in{g}") for g in range(GROUPS)]
        win_in = [sem(f"win_in{c}") for c in range(4)]
        small_in, sel_in, wdn_in, w1_in, w2_in = (sem(n) for n in ("small_in", "sel_in", "wdn_in", "w1_in", "w2_in"))
        x_hi_ready, x0_lo_ready, x_lo_ready = sem("x_hi_ready"), sem("x0_lo_ready"), sem("x_lo_ready")
        w_hi_ready, w0_lo_ready, w_lo_ready = sem("w_hi_ready"), sem("w0_lo_ready"), sem("w_lo_ready")
        w_hi_ready2, w_lo_ready2 = sem("w_hi_ready2"), sem("w_lo_ready2")
        ones_ready, sel_w_ready, sel_hi_ready, sel_p_ready, pad_ready = (sem(n) for n in (
            "ones_ready", "sel_w_ready", "sel_hi_ready", "sel_p_ready", "pad_ready"))
        router_hi_ready, router_lo_ready = sem("router_hi_ready"), sem("router_lo_ready")
        lg_ready, bdiag_ready, logit1_ready, d1_ready, e1_ready = (sem(n) for n in (
            "lg_ready", "bdiag_ready", "logit1_ready", "d1_ready", "e1_ready"))
        w_tok_ready, w_turned, w_row_ready = sem("w_tok_ready"), sem("w_turned"), sem("w_row_ready")
        g_ready, u_ready, wb_ready, y_ready, z_ready, o_ready, logit2_ready, pen_turned = (sem(n) for n in (
            "g_ready", "u_ready", "wb_ready", "y_ready", "z_ready", "o_ready", "logit2_ready", "pen_turned"))
        gate_ready, h_hi_ready, y_hi_ready, r_hi_ready, e2_ready, pen_row_ready = (sem(n) for n in (
            "gate_ready", "h_hi_ready", "y_hi_ready", "r_hi_ready", "e2_ready", "pen_row_ready"))
        act_g_done, gu_done, h_done, y_lo_ready, r_lo_ready, out_done, d2_ready, pen_ready = (sem(n) for n in (
            "act_g_done", "gu_done", "h_done", "y_lo_ready", "r_lo_ready", "out_done", "d2_ready", "pen_ready"))
        pool_act_g_done, last_h_lo_ready, h_lo_ready, step1, step2, stored = (sem(n) for n in (
            "pool_act_g_done", "last_h_lo_ready", "h_lo_ready", "step1", "step2", "stored"))

        POOL_LEAKY = ((0, 2),)

        def leaky_done(g, c):
            if isinstance(g, int) and (g, c) in POOL_LEAKY:
                return pool_act_g_done, POOL_LEAKY.index((g, c)) + 1
            pools = sum(p < (g, c) for p in POOL_LEAKY) if isinstance(g, int) else len(POOL_LEAKY)
            return act_g_done, MC * g + c + 1 - pools

        WIN = ((0, 1), (1, 2), (2, 3), (3, MC))
        LATER = ((wdn_raw, wdn_hi, wdn_lo, wdn_in), (w1_raw, w1_hi, w1_lo, w1_in), (w2_raw, w2_hi, w2_lo, w2_in))

        def piece(w, n):
            return w[:, WIN[n][0] * 256:WIN[n][1] * 256]

        def group(t, g):
            return t[:, bass.ts(g, TOKENS)]

        block = ctx.enter_context(nc.Block())

        @block.sync
        def _(sp):
            def load_x(g):
                sp.dma_start(group(x_raw, g), group(x_t, g)).then_inc(x_in[g], 16)

            def load_w(n):
                sp.dma_start(piece(win_raw, n), piece(w_in, n)).then_inc(win_in[n], 16)

            load_x(0)
            sp.dma_start(small_sb[:, :], small).then_inc(small_in, 16)
            load_w(0)
            sp.dma_start(sel_sb[:, :], select).then_inc(sel_in, 16)
            load_w(1)
            load_x(1)
            load_w(2)
            load_x(2)
            load_w(3)
            load_x(3)
            sp.dma_start(wdn_raw[:, :], w_down).then_inc(wdn_in, 16)
            sp.dma_start(w1_raw[:, :], w1_t).then_inc(w1_in, 16)
            sp.dma_start(w2_raw[:, :], w2_t).then_inc(w2_in, 16)
            with sp.Fori(0, GROUPS) as f:
                sp.wait_ge(out_done, f + 1)
                sp.dma_start(group(out, f), group(y_out, f)).then_inc(stored, 16)
            sp.wait_ge(stored, 16 * GROUPS)

        @block.gpsimd
        def _(pool):
            nc.gpsimd.memset(ones[:, :], 1.0).then_inc(ones_ready, 1)
            nc.gpsimd.memset(pen_row[:, :].bitcast(f32), 1.0).then_inc(ones_ready, 1)
            nc.gpsimd.memset(cand[:, :, NB:], -1.0).then_inc(pad_ready, 1)

            def x_low(g):
                pool.wait_ge(x_hi_ready, g + 1)
                nc.gpsimd.tensor_tensor(group(x_lo, g), group(x_raw, g), group(x_hi, g).bitcast(f32),
                                        ALU.subtract).then_inc(x_lo_ready, 1)

            def w_low(n):
                raw, hi, lo, _ = LATER[n]
                pool.wait_ge(w_hi_ready2, n + 1)
                nc.gpsimd.tensor_tensor(lo[:, :], raw[:, :], hi[:, :].bitcast(f32),
                                        ALU.subtract).then_inc(w_lo_ready2, 1)

            def h_low(g, c):
                pool.wait_ge(h_hi_ready, MC * g + c + 1)
                nc.gpsimd.tensor_tensor(h_lo[:, c, :], h[:, c, :], h_hi[:, c, :].bitcast(f32),
                                        ALU.subtract).then_inc(h_lo_ready, 1)

            def win_low(n):
                pool.wait_ge(w_hi_ready, n + 1)
                nc.gpsimd.tensor_tensor(piece(win_lo, n), piece(win_raw, n), piece(win_hi, n).bitcast(f32),
                                        ALU.subtract).then_inc(w_lo_ready, 1)

            def leaky(g, c):
                pool.wait_ge(gate_ready, MC * g + c + 1)
                nc.gpsimd.tensor_tensor(act_g[:, c, :], gate[:, c, :], act_g[:, c, :],
                                        ALU.subtract).then_inc(pool_act_g_done, 1)

            win_low(1)
            win_low(2)
            x_low(1)
            win_low(3)
            x_low(2)
            x_low(3)
            leaky(0, 2)
            w_low(0)
            for c in range(MC):
                h_low(0, c)
            w_low(1)
            w_low(2)
            with pool.Fori(1, GROUPS - 1) as g:
                for c in range(MC):
                    h_low(g, c)
            for c in range(EC):
                h_low(GROUPS - 1, c)

        @block.scalar
        def _(act):
            def x_high(g):
                act.wait_ge(x_in[g], 16)
                nc.scalar.activation(group(x_hi, g), group(x_raw, g), ACT.Copy).then_inc(x_hi_ready, 1)

            def win_high(n):
                act.wait_ge(win_in[n], 16)
                nc.scalar.activation(piece(win_hi, n), piece(win_raw, n), ACT.Copy).then_inc(w_hi_ready, 1)

            def w_high(n):
                raw, hi, _, loaded = LATER[n]
                act.wait_ge(loaded, 16)
                nc.scalar.activation(hi[:, :], raw[:, :], ACT.Copy).then_inc(w_hi_ready2, 1)

            def exp1(part):
                act.wait_ge(d1_ready, part + 1)
                nc.scalar.activation(e1[:, PART1[part], :], d1[:, PART1[part], :], ACT.Exp,
                                     scale=0.5).then_inc(e1_ready, 1)

            def w_rows(g):
                act.wait_ge(w_turned, g + 1)
                nc.scalar.activation(group(w_row, g), bank[W_ROW_BANKS[g]][0:2 * E, :],
                                     ACT.Copy).then_inc(w_row_ready, 1)

            def gates(g, c, banks=G_BANKS):
                act.wait_ge(g_ready, MC * g + c + 1)
                pools = isinstance(g, int) and (g, c) in POOL_LEAKY
                if pools:
                    if g:
                        act.wait_ge(gu_done, MC * (g - 1) + c + 1)
                    nc.scalar.activation(act_g[:, c, :], bank[banks[c]][:, :], ACT.Relu, scale=-0.01)
                nc.scalar.activation(gate[:, c, :], bank[banks[c]][:, :],
                                     ACT.Relu if pools else ACT.Copy).then_inc(gate_ready, 1)

            def h_high(g, c):
                if c == EC:
                    act.wait_ge(gu_done, MC * (g + 1))
                else:
                    act.wait_ge(h_done, EC * g + c + 1)
                nc.scalar.activation(h_hi[:, c, :], h[:, c, :], ACT.Copy).then_inc(h_hi_ready, 1)

            def y_high(g, y=Y):
                act.wait_ge(y_ready, g + 1)
                nc.scalar.activation(y[0][:, :], y_bank[:, :], ACT.Copy).then_inc(y_hi_ready, 1)

            def exp2(g):
                act.wait_ge(d2_ready, g + 1)
                nc.scalar.activation(e2[:, :, :], d2[:, :, :], ACT.Exp).then_inc(e2_ready, 1)

            def pen_rows(f):
                act.wait_ge(pen_turned, f + 1)
                nc.scalar.activation(pen_row[0:NB, :], turn_bank[0:NB, :], ACT.Copy).then_inc(pen_row_ready, 1)

            def relus(f, c, banks=Z_BANKS):
                act.wait_ge(z_ready, FC * f + c + 1)
                nc.scalar.activation(r_hi[:, c, :], bank[banks[c]][:, :], ACT.Relu).then_inc(r_hi_ready, 1)

            def body(g):
                gates(g, 0)
                h_high(g - 1, EC)
                pen_rows(g - 2)
                relus(g - 2, 0)
                h_high(g, 0)
                relus(g - 2, 1)
                gates(g, 1)
                relus(g - 2, 2)
                relus(g - 2, 3)
                y_high(g - 1)
                h_high(g, 1)
                gates(g, 2)
                h_high(g, 2)
                exp2(g - 1)
                gates(g, 3)
                gates(g, 4)
                h_high(g, 3)

            x_high(0)
            act.wait_ge(small_in, 16)
            nc.scalar.activation(wt_hl[:, 0:E], wt_sb, ACT.Copy).then_inc(router_hi_ready, 1)
            nc.scalar.activation(wr_hl[:, 0:NB], wr_sb, ACT.Copy).then_inc(router_hi_ready, 1)
            win_high(0)
            win_high(1)
            win_high(2)
            x_high(1)
            x_high(2)
            exp1(0)
            win_high(3)
            gates(0, 0, G_BANKS_0)
            x_high(3)
            act.wait_ge(sel_in, 16)
            nc.scalar.activation(sel_w[:, :], sel_sb[0:2 * E, SEL_W:SEL_P], ACT.Copy).then_inc(sel_w_ready, 1)
            gates(0, 1, G_BANKS_0)
            gates(0, 2, G_BANKS_0)
            w_rows(0)
            w_high(0)
            gates(0, 3, G_BANKS_0)
            h_high(0, 0)
            gates(0, 4, G_BANKS_0)
            h_high(0, 1)
            w_high(1)
            h_high(0, 2)
            w_high(2)
            h_high(0, 3)
            exp1(1)
            gates(1, 0, G_BANKS_1)
            h_high(0, 4)
            gates(1, 1, G_BANKS_1)
            gates(1, 2, G_BANKS_1)
            nc.scalar.activation(sel_hi[:, :], sel_sb[:, SEL_P:], ACT.Copy).then_inc(sel_hi_ready, 1)
            y_high(0)
            act.wait_ge(ones_ready, 2)
            w_rows(1)
            gates(1, 3, G_BANKS_1)
            h_high(1, 0)
            w_rows(2)
            h_high(1, 1)
            gates(1, 4, G_BANKS_1)
            w_rows(3)
            h_high(1, 2)
            exp2(0)
            h_high(1, 3)
            with act.Fori(2, GROUPS) as g:
                body(g)
            last_g = GROUPS - 1
            h_high(last_g, EC)
            pen_rows(last_g - 1)
            y_high(last_g, Y_LAST)
            relus(last_g - 1, 0, Z_BANKS_4)
            relus(last_g - 1, 1, Z_BANKS_4)
            relus(last_g - 1, 2, Z_BANKS_4)
            relus(last_g - 1, 3, Z_BANKS_4)
            exp2(last_g)
            pen_rows(last_g)
            for c in range(FC):
                relus(last_g, c, Z_BANKS_5)

        @block.vector
        def _(dve):
            v = nc.vector

            def win_low(n):
                dve.wait_ge(w_hi_ready, n + 1)
                v.tensor_tensor(piece(win_lo, n), piece(win_raw, n), piece(win_hi, n).bitcast(f32),
                                ALU.subtract).then_inc(w0_lo_ready, 1)

            def spread(t, n):
                return t.unsqueeze(2).to_broadcast([128, t.shape[1], n])


            def route(part, n):
                ts = PART1[part]
                tiles = ts.stop - ts.start
                count = iota.unsqueeze(1).to_broadcast([128, tiles, E])

                def after(step):
                    dve.wait_ge(step1, STEPS1 * part + step)

                if n == 0:
                    dve.wait_ge(logit1_ready, part + 1)
                    v.reduce_sum(l1[:, ts, :], logits(L1_BANKS[part], 0, tiles, E).rearrange("p t s e -> p t e s"),
                                 AX.X).then_inc(step1, 1)
                elif n == 1:
                    after(1)
                    v.reduce_max(mx1[:, ts], l1[:, ts, :], AX.X).then_inc(step1, 1)
                elif n == 2:
                    after(2)
                    v.tensor_tensor(d1[:, ts, :], l1[:, ts, :], spread(mx1[:, ts], E), ALU.subtract)\
                        .then_inc(d1_ready, 1)
                elif n == 3:
                    dve.wait_ge(d1_ready, part + 1)
                    v.scalar_tensor_tensor(v1[:, ts, :], d1[:, ts, :], 0.0, count, ALU.is_ge, ALU.mult)\
                        .then_inc(step1, 1)
                elif n == 4:
                    after(3)
                    v.reduce_max(rank1[:, ts], v1[:, ts, :], AX.X).then_inc(step1, 1)
                elif n == 5:
                    after(4)
                    v.tensor_tensor(first[:, ts, :], v1[:, ts, :], spread(rank1[:, ts], E), ALU.is_equal)\
                        .then_inc(step1, 1)
                elif n == 6:
                    dve.wait_ge(e1_ready, part + 1)
                    v.reduce_sum(z1[:, ts], e1[:, ts, :], AX.X).then_inc(step1, 1)
                elif n == 7:
                    after(5)
                    v.scalar_tensor_tensor(e1b[:, ts, :], first[:, ts, :], -2.0, e1[:, ts, :], ALU.mult, ALU.add)\
                        .then_inc(step1, 1)
                elif n == 8:
                    after(7)
                    v.reduce_max(m2nd[:, ts], e1b[:, ts, :], AX.X).then_inc(step1, 1)
                elif n == 9:
                    after(8)
                    v.tensor_tensor(v2[:, ts, :], e1b[:, ts, :], spread(m2nd[:, ts], E), ALU.is_equal)\
                        .then_inc(step1, 1)
                elif n == 10:
                    v.scalar_tensor_tensor(den[:, ts], z1[:, ts], 1e-20, m2nd[:, ts], ALU.mult, ALU.add)\
                        .then_inc(step1, 1)
                elif n == 11:
                    after(9)
                    v.tensor_tensor(v3[:, ts, :], v2[:, ts, :], count, ALU.mult).then_inc(step1, 1)
                elif n == 12:
                    after(10)
                    v.tensor_scalar(den[:, ts], den[:, ts], 1.0, None, ALU.add).then_inc(step1, 1)
                elif n == 13:
                    after(11)
                    v.reduce_max(rank2[:, ts], v3[:, ts, :], AX.X).then_inc(step1, 1)
                elif n == 14:
                    after(12)
                    v.reciprocal(den[:, ts], den[:, ts]).then_inc(step1, 1)
                elif n == 15:
                    after(13)
                    v.tensor_tensor(second[:, ts, :], v3[:, ts, :], spread(rank2[:, ts], E), ALU.is_equal)\
                        .then_inc(step1, 1)
                elif n == 16:
                    after(15)
                    v.tensor_tensor(second[:, ts, :], second[:, ts, :], spread(m2nd[:, ts], E), ALU.mult)\
                        .then_inc(step1, 1)
                elif n == 17:
                    after(16)
                    v.tensor_tensor(wun[:, ts, :], second[:, ts, :], first[:, ts, :], ALU.add).then_inc(step1, 1)
                elif n == 18:
                    after(17)
                    v.tensor_tensor(wgt[:, ts, :], wun[:, ts, :], spread(den[:, ts], E), ALU.mult)\
                        .then_inc(step1, 1)
                elif n == 19:
                    after(18)
                    v.tensor_copy(w_tok[:, ts, 0:E], wgt[:, ts, :]).then_inc(w_tok_ready, 1)
                elif n == 20:
                    dve.wait_ge(w_tok_ready, 2 * part + 1)
                    v.tensor_tensor(w_tok[:, ts, E:], wgt[:, ts, :], w_tok[:, ts, 0:E].bitcast(f32),
                                    ALU.subtract).then_inc(w_tok_ready, 1)

            def leaky(g, c):
                dve.wait_ge(gate_ready, MC * g + c + 1)
                v.scalar_tensor_tensor(act_g[:, c, :], gate[:, c, :], 0.01, gate[:, c, :],
                                       ALU.mult, ALU.max).then_inc(act_g_done, 1)

            def times_up(g, c, banks=U_BANKS):
                dve.wait_ge(u_ready, MC * g + c + 1)
                dve.wait_ge(*leaky_done(g, c))
                v.tensor_tensor(h[:, c, :] if c == EC else gu[:, c, :], bank[banks[c]][:, :],
                                act_g[:, c, :], ALU.mult).then_inc(gu_done, 1)

            def times_weight(g, c, banks=W_BANKS):
                dve.wait_ge(wb_ready, EC * g + c + 1)
                dve.wait_ge(gu_done, MC * g + c + 1)
                v.tensor_tensor(h[:, c, :], bank[banks[c]][:, :], gu[:, c, :], ALU.mult).then_inc(h_done, 1)

            def y_low(g, y=Y):
                dve.wait_ge(y_hi_ready, g + 1)
                v.tensor_tensor(y[1][:, :], y_bank[:, :], y[0][:, :].bitcast(f32),
                                ALU.subtract).then_inc(y_lo_ready, 1)

            def relu_low(f, c, banks=Z_BANKS):
                dve.wait_ge(r_hi_ready, FC * f + c + 1)
                v.scalar_tensor_tensor(r_lo[:, c, :], bank[banks[c]][:, :], 0.0, r_hi[:, c, :].bitcast(f32),
                                       ALU.max, ALU.subtract).then_inc(r_lo_ready, 1)

            def result(f, bank=o_bank):
                dve.wait_ge(o_ready, f + 1)
                v.scalar_tensor_tensor(group(y_out, f), bank[:, :], b2_sb, group(x_raw, f),
                                       ALU.add, ALU.add).then_inc(out_done, 1)

            STEPS2 = 9

            def before_max(g):
                dve.wait_ge(step2, STEPS2 * g + 6)

            def before_replace(g):
                dve.wait_ge(step2, STEPS2 * g + 8)

            def pick(g, n, b=4):
                if n == 0:
                    dve.wait_ge(logit2_ready, g + 1)
                    v.reduce_sum(l2[:, :, :], logits(b, 0, TG, NB).rearrange("p t s e -> p t e s"), AX.X)\
                        .then_inc(step2, 1)
                elif n == 1:
                    dve.wait_ge(step2, STEPS2 * g + 1)
                    v.reduce_max(mx2[:, :], l2[:, :, :], AX.X).then_inc(step2, 1)
                elif n == 2:
                    dve.wait_ge(step2, STEPS2 * g + 2)
                    v.tensor_tensor(d2[:, :, :], l2[:, :, :], spread(mx2[:, :], NB), ALU.subtract)\
                        .then_inc(d2_ready, 1)
                elif n == 3:
                    dve.wait_ge(e2_ready, g + 1)
                    v.reduce_sum(z2[:, :], e2[:, :, :], AX.X).then_inc(step2, 1)
                elif n == 4:
                    dve.wait_ge(step2, STEPS2 * g + 3)
                    v.reciprocal(rz2[:, :], z2[:, :]).then_inc(step2, 1)
                elif n == 5:
                    dve.wait_ge(step2, STEPS2 * g + 4)
                    v.tensor_tensor(s2[:, :, :], e2[:, :, :], spread(rz2[:, :], NB), ALU.mult).then_inc(step2, 1)
                elif n == 6:
                    dve.wait_ge(step2, STEPS2 * g + 5)
                    v.scalar_tensor_tensor(cand[:, :, 0:NB], s2[:, :, :], TINY, s2[:, :, :],
                                           ALU.is_ge, ALU.mult).then_inc(step2, 1)
                elif n == 7:
                    if isinstance(g, int):
                        before_max(g)
                    for t in range(TG):
                        last = v.max(top8[:, t, :], cand[:, t, 0:NB])
                    last.then_inc(step2, 1)
                elif n == 8:
                    dve.wait_ge(step2, STEPS2 * g + 7)
                    v.memset(top8[:, :, TOP2:], -1.0).then_inc(step2, 1)
                elif n == 9:
                    if isinstance(g, int):
                        before_replace(g)
                    for t in range(TG):
                        last = v.match_replace(rest[:, t, :], top8[:, t, :], cand[:, t, :], 2.0)
                    last.then_inc(step2, 1)
                elif n == 10:
                    dve.wait_ge(step2, STEPS2 * g + 9)
                    v.tensor_scalar(pen[:, :, :], rest[:, :, 0:NB], 2.0, PENALTY,
                                    ALU.is_lt, ALU.mult).then_inc(pen_ready, 1)

            def chunk(g, c):
                leaky(g, c)
                times_up(g, c)
                if c < EC:
                    times_weight(g, c)

            def body(g):
                chunk(g, 0)
                relu_low(g - 2, 0)
                relu_low(g - 2, 1)
                chunk(g, 1)
                relu_low(g - 2, 2)
                relu_low(g - 2, 3)
                y_low(g - 1)
                chunk(g, 2)
                for n in range(3):
                    pick(g - 1, n)
                leaky(g, 3)
                pick(g - 1, 3)
                times_up(g, 3)
                pick(g - 1, 4)
                pick(g - 1, 5)
                times_weight(g, 3)
                pick(g - 1, 6)
                before_max(g - 1)
                result(g - 2)
                pick(g - 1, 7)
                pick(g - 1, 8)
                before_replace(g - 1)
                leaky(g, 4)
                pick(g - 1, 9)
                times_up(g, 4)
                pick(g - 1, 10)

            dve.wait_ge(router_hi_ready, 2)
            v.tensor_tensor(wt_hl[:, E:], wt_sb, wt_hl[:, 0:E].bitcast(f32), ALU.subtract)
            v.tensor_tensor(wr_hl[:, NB:], wr_sb, wr_hl[:, 0:NB].bitcast(f32),
                            ALU.subtract).then_inc(router_lo_ready, 1)
            dve.wait_ge(x_hi_ready, 1)
            v.tensor_tensor(group(x_lo, 0), group(x_raw, 0), group(x_hi, 0).bitcast(f32),
                            ALU.subtract).then_inc(x0_lo_ready, 1)
            win_low(0)
            dve.wait_ge(sel_in, 16)
            dve.wait_ge(lg_ready, 1)
            v.tensor_tensor(bdiag[:, :, :], o_bank[0:B, 0:E].unsqueeze(1).to_broadcast([B, B, E]),
                            sel_sb[0:B, DIAG:SEL_W].rearrange("p (t e) -> p t e", e=E),
                            ALU.mult).then_inc(bdiag_ready, 1)
            for n in range(9):
                route(0, n)
            leaky(0, 0)
            for n in range(9, 16):
                route(0, n)
            times_up(0, 0, U_BANKS_0)
            for n in range(16, 21):
                route(0, n)
            leaky(0, 1)
            times_up(0, 1, U_BANKS_0)
            times_weight(0, 0, W_BANKS_0)
            times_up(0, 2, U_BANKS_0)
            times_weight(0, 1, W_BANKS_0)
            leaky(0, 3)
            times_up(0, 3, U_BANKS_0)
            times_weight(0, 2, W_BANKS_0)
            leaky(0, 4)
            times_up(0, 4, U_BANKS_0)
            times_weight(0, 3, W_BANKS_0)
            for n in range(7):
                route(1, n)
            leaky(1, 0)
            for n in range(7, 12):
                route(1, n)
            times_up(1, 0)
            for n in range(12, 17):
                route(1, n)
            leaky(1, 1)
            for n in range(17, 21):
                route(1, n)
            times_up(1, 1)
            dve.wait_ge(pad_ready, 1)
            leaky(1, 2)
            times_up(1, 2)
            y_low(0)
            times_weight(1, 0, W_BANKS_1)
            times_weight(1, 1, W_BANKS_1)
            leaky(1, 3)
            pick(0, 0, 6)
            times_up(1, 3)
            pick(0, 1)
            times_weight(1, 2, W_BANKS_1)
            pick(0, 2)
            leaky(1, 4)
            pick(0, 3)
            dve.wait_ge(sel_hi_ready, 1)
            v.scalar_tensor_tensor(sel_p[:, :], sel_hi[:, :].bitcast(f32), sel_sb[:, NEG:BR], sel_sb[:, SEL_P:],
                                   ALU.mult, ALU.add).then_inc(sel_p_ready, 1)
            pick(0, 4)
            times_weight(1, 3, W_BANKS_1)
            pick(0, 5)
            times_up(1, 4)
            for n in range(6, 11):
                pick(0, n)
            with dve.Fori(2, GROUPS) as g:
                body(g)
            last_g = GROUPS - 1
            dve.wait_ge(h_hi_ready, MC * GROUPS)
            v.tensor_tensor(h_lo[:, EC, :], h[:, EC, :], h_hi[:, EC, :].bitcast(f32),
                            ALU.subtract).then_inc(last_h_lo_ready, 1)
            y_low(last_g, Y_LAST)
            relu_low(last_g - 1, 0, Z_BANKS_4)
            relu_low(last_g - 1, 1, Z_BANKS_4)
            for n in range(3):
                pick(last_g, n)
            relu_low(last_g - 1, 2, Z_BANKS_4)
            pick(last_g, 3)
            pick(last_g, 4)
            relu_low(last_g - 1, 3, Z_BANKS_4)
            for n in range(5, 7):
                pick(last_g, n)
            for n in range(7, 11):
                pick(last_g, n)
            result(last_g - 1)
            for c in range(FC):
                relu_low(last_g, c, Z_BANKS_5)
            result(last_g, y_bank)

        @block.tensor
        def _(pe):
            def product(dst, w_hi, w_lo, m_hi, m_lo, start, stop):
                nc.tensor.matmul(dst, w_hi, m_hi, start=start, stop=False)
                nc.tensor.matmul(dst, w_lo, m_hi, start=False, stop=False)
                return nc.tensor.matmul(dst, w_hi, m_lo, start=False, stop=stop)

            def tile_logits(b, n, place, tile, hi, lo, w_hl):
                at = slice(tile * 128, (tile + 1) * 128)
                to = place * 2 * n
                nc.tensor.matmul(bank[b][:, to:to + 2 * n], hi[:, at], w_hl[:, :],
                                 start=(place == 0), stop=False, skip_group_check=True)
                nc.tensor.matmul(bank[b][:, to:to + n], lo[:, at], w_hl[:, 0:n],
                                 start=False, stop=False, skip_group_check=True)

            def route_group(part, g):
                pe.wait_ge(x_hi_ready, g + 1)
                if g:
                    pe.wait_ge(x_lo_ready, g)
                else:
                    pe.wait_ge(x0_lo_ready, 1)
                for t in range(g * TG, (g + 1) * TG):
                    tile_logits(L1_BANKS[part], E, t - PART1[part].start, t, x_hi, x_lo, wt_hl)

            def route_condition(part):
                ts = PART1[part]
                nc.tensor.matmul(logits(L1_BANKS[part], 0, ts.stop - ts.start, E)[:, :, 0, :], ones[:, :],
                                 bdiag[:, ts, :], start=False, stop=True,
                                 skip_group_check=True).then_inc(logit1_ready, 1)

            def turn_weights(g):
                for t in range(TG):
                    last = nc.tensor.transpose(bank[W_ROW_BANKS[g]][0:2 * E, t * 128:(t + 1) * 128],
                                               w_tok[:, g * TG + t, :].bitcast(f32), ident)
                last.then_inc(w_turned, 1)

            def weights_in(c, up):
                at = (2 * c + up) * 128
                return win_hi[:, at:at + 128], win_lo[:, at:at + 128]

            def gate_product(g, c, banks=G_BANKS):
                product(bank[banks[c]][:, :], *weights_in(c, 0), group(x_hi, g), group(x_lo, g),
                        True, True).then_inc(g_ready, 1)

            def up_product(g, c, banks=U_BANKS):
                product(bank[banks[c]][:, :], *weights_in(c, 1), group(x_hi, g), group(x_lo, g),
                        True, True).then_inc(u_ready, 1)

            def weight_product(g, c, banks=W_BANKS):
                nc.tensor.matmul(bank[banks[c]][:, :], sel_w[:, c * 128:(c + 1) * 128], group(w_row, g),
                                 start=True, stop=True).then_inc(wb_ready, 1)

            def loop_gate(g, c):
                pe.wait_ge(gate_ready, MC * g + c)
                gate_product(g, c)

            def loop_up(g, c):
                (hi, lo), up = weights_in(c, 1), bank[U_BANKS[c]]
                nc.tensor.matmul(up[:, :], hi, group(x_hi, g), start=True, stop=False)
                nc.tensor.matmul(up[:, :], lo, group(x_hi, g), start=False, stop=False)
                if c < EC:
                    pe.wait_ge(h_done, EC * g + c)
                nc.tensor.matmul(up[:, :], hi, group(x_lo, g), start=False, stop=True).then_inc(u_ready, 1)
                if c < EC:
                    weight_product(g, c)

            def chunk(g, c):
                loop_gate(g, c)
                loop_up(g, c)

            def down(g, c):
                at = slice(c * 128, (c + 1) * 128)
                pe.wait_ge(h_hi_ready, MC * g + c + 1)
                nc.tensor.matmul(y_bank[:, :], wdn_hi[:, at], h_hi[:, c, :], start=(c == 0), stop=False)
                nc.tensor.matmul(y_bank[:, :], wdn_lo[:, at], h_hi[:, c, :], start=False, stop=False)
                if isinstance(g, int) and (g, c) == (GROUPS - 1, EC):
                    pe.wait_ge(last_h_lo_ready, 1)
                else:
                    pe.wait_ge(h_lo_ready, MC * g + c + 1)
                last = nc.tensor.matmul(y_bank[:, :], wdn_hi[:, at], h_lo[:, c, :], start=False, stop=(c == MC - 1))
                if c == MC - 1:
                    last.then_inc(y_ready, 1)

            def router2(g, y=Y, b=4):
                pe.wait_ge(y_hi_ready, g + 1)
                pe.wait_ge(y_lo_ready, g + 1)
                for t in range(TG):
                    tile_logits(b, NB, t, t, *y, wr_hl)
                nc.tensor.matmul(logits(b, 0, TG, NB)[:, :, 0, :], ones[0:1, :],
                                 sel_sb[0:1, BR:DIAG].unsqueeze(1).to_broadcast([1, TG, NB]),
                                 start=False, stop=True, skip_group_check=True).then_inc(logit2_ready, 1)

            def turn_penalties(f):
                pe.wait_ge(pen_ready, f + 1)
                for t in range(TG):
                    last = nc.tensor.transpose(turn_bank[0:NB, t * 128:(t + 1) * 128], pen[:, t, :], ident)
                last.then_inc(pen_turned, 1)

            def ffn_up(c, banks=Z_BANKS, y=Y):
                at = slice(c * 128, (c + 1) * 128)
                product(bank[banks[c]][:, :], w1_hi[:, at], w1_lo[:, at], y[0][:, :], y[1][:, :], True, False)

            def penalise(c, banks=Z_BANKS):
                nc.tensor.matmul(bank[banks[c]][:, :], sel_p[:, c * 128:(c + 1) * 128], pen_row[:, :],
                                 start=False, stop=True).then_inc(z_ready, 1)

            def ffn_down_hi(f, c, bank=o_bank):
                at = slice(c * 128, (c + 1) * 128)
                pe.wait_ge(r_hi_ready, FC * f + c + 1)
                nc.tensor.matmul(bank[:, :], w2_hi[:, at], r_hi[:, c, :], start=(c == 0), stop=False)
                nc.tensor.matmul(bank[:, :], w2_lo[:, at], r_hi[:, c, :], start=False, stop=False)

            def ffn_down_lo(f, c, bank=o_bank):
                at = slice(c * 128, (c + 1) * 128)
                pe.wait_ge(r_lo_ready, FC * f + c + 1)
                last = nc.tensor.matmul(bank[:, :], w2_hi[:, at], r_lo[:, c, :], start=False, stop=(c == FC - 1))
                if c == FC - 1:
                    last.then_inc(o_ready, 1)

            def ffn_down(f, c):
                ffn_down_hi(f, c)
                ffn_down_lo(f, c)

            def body(g):
                f = g - 2
                chunk(g, 0)
                down(g - 1, 3)
                turn_penalties(f)
                pe.wait_ge(gu_done, MC * g)
                ffn_up(0)
                loop_gate(g, 1)
                pe.wait_ge(pen_row_ready, f + 1)
                ffn_up(1)
                penalise(0)
                penalise(1)
                loop_up(g, 1)
                down(g - 1, 4)
                for c in (2, 3):
                    pe.wait_ge(r_lo_ready, FC * f + c - 1)
                    ffn_up(c)
                    penalise(c)
                chunk(g, 2)
                ffn_down(f, 0)
                ffn_down(f, 1)
                router2(g - 1)
                chunk(g, 3)
                down(g, 0)
                ffn_down(f, 2)
                ffn_down(f, 3)
                chunk(g, 4)
                down(g, 1)
                down(g, 2)

            pe.wait_ge(small_in, 16)
            nc.tensor.matmul(o_bank[0:B, 0:E], cond_sb, wg_sb, start=True, stop=True).then_inc(lg_ready, 1)
            pe.wait_ge(router_lo_ready, 1)
            pe.wait_ge(ones_ready, 1)
            route_group(0, 0)
            pe.wait_ge(bdiag_ready, 1)
            route_condition(0)
            pe.wait_ge(w0_lo_ready, 1)
            gate_product(0, 0, G_BANKS_0)
            up_product(0, 0, U_BANKS_0)
            pe.wait_ge(w_lo_ready, 1)
            gate_product(0, 1, G_BANKS_0)
            up_product(0, 1, U_BANKS_0)
            pe.wait_ge(w_lo_ready, 2)
            pe.wait_ge(gate_ready, 1)
            gate_product(0, 2, G_BANKS_0)
            pe.wait_ge(w_tok_ready, 2)
            turn_weights(0)
            up_product(0, 2, U_BANKS_0)
            pe.wait_ge(w_row_ready, 1)
            pe.wait_ge(sel_w_ready, 1)
            weight_product(0, 0, W_BANKS_0)
            weight_product(0, 1, W_BANKS_0)
            pe.wait_ge(w_lo_ready, 3)
            pe.wait_ge(gate_ready, 2)
            gate_product(0, 3, G_BANKS_0)
            pe.wait_ge(gu_done, 1)
            up_product(0, 3, U_BANKS_0)
            route_group(1, 1)
            pe.wait_ge(h_done, 1)
            weight_product(0, 2, W_BANKS_0)
            pe.wait_ge(gate_ready, 3)
            gate_product(0, 4, G_BANKS_0)
            route_group(1, 2)
            pe.wait_ge(gu_done, 2)
            up_product(0, 4, U_BANKS_0)
            pe.wait_ge(h_done, 2)
            weight_product(0, 3, W_BANKS_0)
            route_group(1, 3)
            route_condition(1)
            pe.wait_ge(gate_ready, 4)
            gate_product(1, 0, G_BANKS_1)
            pe.wait_ge(gu_done, 4)
            up_product(1, 0)
            pe.wait_ge(gate_ready, 5)
            gate_product(1, 1, G_BANKS_1)
            pe.wait_ge(gu_done, 5)
            up_product(1, 1)
            pe.wait_ge(w_lo_ready2, 1)
            pe.wait_ge(step1, STEPS1 + 1)
            down(0, 0)
            down(0, 1)
            pe.wait_ge(gate_ready, 6)
            gate_product(1, 2, G_BANKS_1)
            pe.wait_ge(gu_done, 6)
            up_product(1, 2)
            for c in range(2, MC):
                down(0, c)
            pe.wait_ge(w_tok_ready, 4)
            turn_weights(1)
            pe.wait_ge(gate_ready, 7)
            gate_product(1, 3, G_BANKS_1)
            pe.wait_ge(w_row_ready, 2)
            pe.wait_ge(h_done, 4)
            weight_product(1, 0, W_BANKS_1)
            weight_product(1, 1, W_BANKS_1)
            router2(0, b=6)
            turn_weights(2)
            pe.wait_ge(gu_done, 7)
            up_product(1, 3)
            pe.wait_ge(h_done, 5)
            weight_product(1, 2, W_BANKS_1)
            pe.wait_ge(gate_ready, 8)
            gate_product(1, 4, G_BANKS_1)
            pe.wait_ge(w_row_ready, 3)
            turn_weights(3)
            pe.wait_ge(h_done, 6)
            weight_product(1, 3, W_BANKS_1)
            pe.wait_ge(w_row_ready, 4)
            up_product(1, 4)
            pe.wait_ge(step2, 1)
            down(1, 0)
            down(1, 1)
            down(1, 2)
            pe.wait_ge(w_row_ready, GROUPS)
            pe.wait_ge(sel_p_ready, 1)
            pe.wait_ge(w_lo_ready2, 3)
            with pe.Fori(2, GROUPS) as g:
                body(g)
            g = GROUPS - 1
            f = g - 1
            ffn_up(0, Z_BANKS_4)
            pe.wait_ge(h_done, EC * GROUPS)
            ffn_up(1, Z_BANKS_4)
            down(g, 3)
            pe.wait_ge(gate_ready, MC * GROUPS)
            ffn_up(2, Z_BANKS_4)
            turn_penalties(f)
            down(g, 4)
            pe.wait_ge(pen_row_ready, f + 1)
            for c in range(3):
                penalise(c, Z_BANKS_4)
            ffn_up(3, Z_BANKS_4)
            penalise(3, Z_BANKS_4)
            router2(g, Y_LAST)
            ffn_down(f, 0)
            ffn_down(f, 1)
            f = g
            ffn_up(0, Z_BANKS_5, Y_LAST)
            for c in range(1, FC):
                pe.wait_ge(r_lo_ready, FC * (f - 1) + c)
                ffn_up(c, Z_BANKS_5, Y_LAST)
            ffn_down(f - 1, 2)
            turn_penalties(f)
            ffn_down(f - 1, 3)
            pe.wait_ge(pen_row_ready, f + 1)
            for c in range(FC):
                penalise(c, Z_BANKS_5)
            for c in range(FC):
                ffn_down_hi(f, c, y_bank)
            for c in range(FC):
                ffn_down_lo(f, c, y_bank)


def kernel(x, cond_64, L0_cond_wt, L0_cond_wg, L0_cond_w_gate, L0_cond_w_up, L0_cond_w_down, L0_cond_sw_gate,
           L0_cond_sw_up, L0_cond_sw_down, L0_ffn_w_router, L0_ffn_b_router, L0_ffn_w1, L0_ffn_b1, L0_ffn_w2,
           L0_ffn_b2):
    import numpy as np
    import concourse.bacc as bacc
    from concourse.bass_utils import run_bass_kernel_spmd

    def arr(a):
        return np.asarray(a)

    def columns(w):
        return arr(w).transpose(1, 0, 2).reshape(D, E * M)

    def rows(a, n):
        return np.pad(a, ((0, n - a.shape[0]), (0, 0)))

    gate = np.concatenate([columns(L0_cond_w_gate), arr(L0_cond_sw_gate)], 1).reshape(D, MC, 1, 128)
    up = np.concatenate([columns(L0_cond_w_up), arr(L0_cond_sw_up)], 1).reshape(D, MC, 1, 128)
    w_down = np.concatenate([arr(L0_cond_w_down).reshape(E * M, D), arr(L0_cond_sw_down)], 0)
    identity = np.eye(128, dtype=np.float32)
    descending = np.broadcast_to(np.arange(E, 0, -1, dtype=np.float32), (128, E))
    minus_last = np.zeros((NB + 2, 1), np.float32)
    minus_last[-1] = -1
    diagonal = np.repeat(np.eye(B, dtype=np.float32), E, axis=1)
    expert_of = np.tile(np.repeat(np.eye(E, dtype=np.float32), M, axis=1), (2, 1))
    block_of = np.repeat(np.eye(NB, dtype=np.float32), HID // NB, axis=1)
    b1 = arr(L0_ffn_b1).reshape(1, HID)
    arrays = {
        "x_t": arr(x).reshape(N_TOK, D).T,
        "w_in": np.concatenate([gate, up], 2).reshape(D, 2 * MC * 128),
        "w_down": w_down.reshape(MC, 128, D).transpose(1, 0, 2).reshape(128, MC * D),
        "w1_t": arr(L0_ffn_w1).T,
        "w2_t": arr(L0_ffn_w2).T.reshape(FC, 128, D).transpose(1, 0, 2).reshape(128, FC * D),
        "small": np.concatenate([identity, descending, arr(L0_cond_wt).T, arr(L0_ffn_w_router),
                                 arr(L0_ffn_b2).reshape(D, 1), rows(arr(L0_cond_wg).T, 128),
                                 rows(arr(cond_64).T, 128)], 1),
        "select": np.concatenate([minus_last, rows(arr(L0_ffn_b_router).reshape(1, NB), NB + 2),
                                  rows(diagonal, NB + 2), rows(expert_of, NB + 2),
                                  np.concatenate([block_of, b1, b1], 0)], 1),
    }
    nc = bacc.Bacc("TRN2", target_bir_lowering=False, num_devices=1)
    arrays = {n: np.ascontiguousarray(a) for n, a in arrays.items()}
    args = [nc.dram_tensor(n, a.shape, mybir.dt.from_np(a.dtype), kind="ExternalInput").ap()
            for n, a in arrays.items()]
    args.append(nc.dram_tensor("out", (D, N_TOK), mybir.dt.float32, kind="ExternalOutput").ap())
    build(nc, *args)
    r = run_bass_kernel_spmd(nc, [arrays], core_ids=[0])
    return r.results[0]["out"].T.reshape(16, 128, 128)
```
